# Optimizing a Trainium2 kernel written in Bass

```python
import numpy as np
import jax
import jax.numpy as jnp

def _softmax(x, axis=-1):
    return jax.nn.softmax(x, axis=axis)

def _gelu(x):
    return jax.nn.gelu(x, approximate=True)

def _silu(x):
    return jax.nn.silu(x)

def _sigmoid(x):
    return jax.nn.sigmoid(x)

def _layernorm(x, axis=-1, eps=1e-05):
    m = jnp.mean(x, axis=axis, keepdims=True)
    v = jnp.var(x, axis=axis, keepdims=True)
    return (x - m) / jnp.sqrt(v + eps)

def _scatter_add(tgt, idx, src, axis=0):
    return tgt.at[idx].add(src)

def _segment_sum(src, seg, n):
    return jax.ops.segment_sum(src, seg, n)
kernel_name = 'mk_seq_postln_d1_jaxref_r4_0efc3c'

def setup_inputs(seed: int=0):
    np.random.seed(seed)
    _w = jnp.asarray

    def _L0_attn_setup():
        import jax, jax.numpy as jnp
        import numpy as np
        key = jax.random.key(seed)
        ks = jax.random.split(key, 6)
        B, T, D, N = (8, 1024, 256, 16)
        s = 0.02
        return {'x': jax.random.normal(ks[0], (B, T, D), jnp.float32), 'Wd': jax.random.normal(ks[1], (D, D), jnp.float32) * s, 'bd': jnp.zeros((D,), jnp.float32), 'Wb': jax.random.normal(ks[2], (D, N), jnp.float32) * s, 'bb': jnp.zeros((N,), jnp.float32), 'Wc': jax.random.normal(ks[3], (D, N), jnp.float32) * s, 'bc': jnp.zeros((N,), jnp.float32), 'Wo': jax.random.normal(ks[4], (D, D), jnp.float32) * s, 'bo': jnp.zeros((D,), jnp.float32), 'A': jax.random.normal(ks[5], (D, N), jnp.float32) * 0.01}
    _L0_attn_in = _L0_attn_setup()

    def _L0_ffn_setup():
        import jax, jax.numpy as jnp
        import numpy as np
        B, S, H, I, E = (2, 1024, 256, 128, 8)
        key = jax.random.key(seed)
        ks = jax.random.split(key, 5)
        scale_h = 1.0 / np.sqrt(H)
        scale_i = 1.0 / np.sqrt(I)
        return {'hidden_states': jax.random.normal(ks[0], (B, S, H), dtype=jnp.float32), 'gate_w': jax.random.normal(ks[1], (E, H), dtype=jnp.float32) * scale_h, 'w_gate': jax.random.normal(ks[2], (E, I, H), dtype=jnp.float32) * scale_h, 'w_up': jax.random.normal(ks[3], (E, I, H), dtype=jnp.float32) * scale_h, 'w_down': jax.random.normal(ks[4], (E, H, I), dtype=jnp.float32) * scale_i}
    _L0_ffn_in = _L0_ffn_setup()
    _d = {'L0_attn_x': _L0_attn_in['x'], 'L0_attn_Wd': _L0_attn_in['Wd'], 'L0_attn_bd': _L0_attn_in['bd'], 'L0_attn_Wb': _L0_attn_in['Wb'], 'L0_attn_bb': _L0_attn_in['bb'], 'L0_attn_Wc': _L0_attn_in['Wc'], 'L0_attn_bc': _L0_attn_in['bc'], 'L0_attn_Wo': _L0_attn_in['Wo'], 'L0_attn_bo': _L0_attn_in['bo'], 'L0_attn_A': _L0_attn_in['A'], 'L0_ffn_gate_w': _L0_ffn_in['gate_w'], 'L0_ffn_w_gate': _L0_ffn_in['w_gate'], 'L0_ffn_w_up': _L0_ffn_in['w_up'], 'L0_ffn_w_down': _L0_ffn_in['w_down']}
    _x0 = _d['L0_attn_x']
    _d['L0_attn_x'] = jax.random.normal(jax.random.fold_in(jax.random.key(seed), 1), (4, 1024, 256), dtype=_x0.dtype)
    del _x0
    return _d

def reference(L0_attn_x, L0_attn_Wd, L0_attn_bd, L0_attn_Wb, L0_attn_bb, L0_attn_Wc, L0_attn_bc, L0_attn_Wo, L0_attn_bo, L0_attn_A, L0_ffn_gate_w, L0_ffn_w_gate, L0_ffn_w_up, L0_ffn_w_down):

    def _L0_attn_ref(x, Wd, bd, Wb, bb, Wc, bc, Wo, bo, A):
        import jax, jax.numpy as jnp
        import numpy as np
        delta = jax.nn.softplus(x @ Wd + bd)
        dbar = jnp.mean(delta, axis=-1, keepdims=True)
        Bt = x @ Wb + bb
        Ct = x @ Wc + bc
        sA = jax.nn.sigmoid(jnp.mean(A, axis=0))
        a = 1.0 - dbar
        b = dbar * Bt * sA

        def step(h, ab):
            at, bt = ab
            h = h * at + bt
            return (h, h)
        h0 = jnp.zeros((x.shape[0], A.shape[1]), x.dtype)
        _, hs = jax.lax.scan(step, h0, (jnp.swapaxes(a, 0, 1), jnp.swapaxes(b, 0, 1)))
        hs = jnp.swapaxes(hs, 0, 1)
        y = jnp.sum(hs * Ct, axis=-1, keepdims=True) * x
        return y @ Wo + bo

    def _L0_ffn_ref(hidden_states, gate_w, w_gate, w_up, w_down):
        import jax, jax.numpy as jnp
        import numpy as np
        B, S, H, I, E = (2, 1024, 256, 128, 8)
        b, s, h = hidden_states.shape
        x = hidden_states.reshape(-1, h)
        logits = x @ gate_w.T
        top_v = jnp.max(logits, axis=-1)
        sel = jnp.argmax(logits, axis=-1)
        rw = jax.nn.sigmoid(top_v)
        out = jnp.zeros_like(x)
        n_exp = gate_w.shape[0]
        for e in range(n_exp):
            mask = (sel == e).astype(x.dtype)
            xs = x * (rw * mask)[:, None]
            g = xs @ w_gate[e].T
            u = xs @ w_up[e].T
            out = out + u * jax.nn.silu(g) @ w_down[e].T
        return out.reshape(b, s, h)
    x = L0_attn_x
    x = _layernorm(x + _L0_attn_ref(x, L0_attn_Wd, L0_attn_bd, L0_attn_Wb, L0_attn_bb, L0_attn_Wc, L0_attn_bc, L0_attn_Wo, L0_attn_bo, L0_attn_A), axis=-1)
    x = _layernorm(x + _L0_ffn_ref(x, L0_ffn_gate_w, L0_ffn_w_gate, L0_ffn_w_up, L0_ffn_w_down), axis=-1)
    return x

_drawn_inputs = setup_inputs


def setup_inputs(seed=0):
    import zlib

    import numpy as np

    out = dict(_drawn_inputs(seed))
    spreads = {'L0_attn_bd': (0.0, 0.1),
     'L0_attn_bb': (0.0, 0.1),
     'L0_attn_bc': (0.0, 0.1),
     'L0_attn_bo': (0.0, 0.1)}
    factors = {}
    for name, (base, spread) in spreads.items():
        noise = np.random.default_rng([zlib.crc32(name.encode()), seed]).standard_normal(out[name].shape)
        drawn = base * np.exp(spread * noise) if base else spread * noise
        out[name] = jnp.asarray(drawn.astype(out[name].dtype))
    for name, factor in factors.items():
        out[name] = (out[name] * factor).astype(out[name].dtype)
    return out
```

```python
import concourse.bass as bass
from concourse import mybir
from contextlib import ExitStack


class Step:

    def __init__(self, turn, c, ring):
        self.turn, self.c, self.ring = turn, c, ring
        self.n = turn * ring + c
        self.slot = c % ring
        self.round = turn + c // ring

    def plus(self, d):
        return Step(self.turn, self.c + d, self.ring)

    def within(self, lo, hi):
        return not isinstance(self.n, int) or lo <= self.n < hi


def run_steps(engine, body, first, loop_from, loop_to, last, ring):
    for n in range(first, loop_from):
        body(Step(0, n, ring))
    if loop_to > loop_from:
        with engine.Fori(0, (loop_to - loop_from) // ring) as turn:
            for u in range(ring):
                body(Step(turn, loop_from + u, ring))
    for n in range(loop_to, last):
        body(Step(0, n, ring))


def wait(engine, sem, value):
    if not isinstance(value, int) or value > 0:
        engine.wait_ge(sem, value)


def ssm_attention_then_top1_moe(nc: bass.Bass, x, xt, wd, wb, wc, wo, wot, bd, bb, bc, bo, bo_cols, a_mat, gwt, wgu, wdn, out):
    fp32, fp32r, i32 = mybir.dt.float32, mybir.dt.float32r, mybir.dt.int32
    ALU = mybir.AluOpType
    ACT = mybir.ActivationFunctionType
    X_AXIS = mybir.AxisListType.X

    P = 128
    NB, T, D = x.shape
    N = wb.shape[1]
    E = gwt.shape[1]
    F = wdn.shape[1]
    KC = D // P
    CH = T // P
    TILES = CH * NB
    TOK = NB * T
    Q = NB * N
    ZS = D + 2 * N + 2 * E
    G0 = D + 2 * N
    ROW = D + 2
    ST = TILES + E - 1
    EPS = 1e-5
    NO_TOKEN = 1 << 20
    R1, R2 = 2, 8

    ctx = ExitStack()
    with ctx:
        def sb(name, shape, dt=fp32):
            return ctx.enter_context(nc.sbuf_tensor(name, shape, dt))

        def sem(name):
            return ctx.enter_context(nc.semaphore(name))

        wz = sb("wz", [P, KC, ZS])
        wz_hi, wz_lo = sb("wz_hi", [P, KC, ZS], fp32r), sb("wz_lo", [P, KC, ZS], fp32r)
        wo_f = sb("wo_f", [P, KC, D])
        wo_hi, wo_lo = sb("wo_hi", [P, KC, D], fp32r), sb("wo_lo", [P, KC, D], fp32r)
        wot_f, gwt_f, bogw = sb("wot_f", [P, KC, D]), sb("gwt_f", [P, KC, E]), sb("bogw", [P, KC, E])
        bo_col = sb("bo_col", [P, KC])
        bo_row = sb("bo_row", [P, D])
        bias_f, bias_hl = sb("bias_f", [2, ZS]), sb("bias_hl", [P, ZS], fp32r)
        two_ones = sb("two_ones", [P, P], fp32r)
        a4 = sb("a4", [P, KC, NB, N])
        ident, ones, below = sb("ident", [P, P]), sb("ones", [P, P]), sb("below", [P, P])
        batch_sel = sb("batch_sel", [Q, NB])
        sig_a = sb("sig_a", [Q, 2])
        gate_sum = sb("gate_sum", [P, E])
        falling = sb("falling", [P, E])
        falling_i = sb("falling_i", [P, E], i32)
        tile_no, tile_no_i = sb("tile_no", [1, ST]), sb("tile_no_i", [1, ST], i32)
        keep = sb("keep", [P, E, TILES])
        minus_half = sb("minus_half", [P, NB])
        empty_row = sb("empty_row", [P, ROW])
        w_gu, w_dn = sb("w_gu", [P, E, KC, 2 * F]), sb("w_dn", [P, E, D])

        xr, xts = sb("xr", [P, R1, NB, D]), sb("xts", [P, R1, KC, NB * P])
        xh, xl = sb("xh", [P, R1, KC, NB * P], fp32r), sb("xl", [P, R1, KC, NB * P], fp32r)
        xbo = sb("xbo", [P, R1, NB, D])
        zs = sb("zs", [P, R1, NB, ZS])
        az = sb("az", [P, R1, NB, D])
        relu_z = sb("relu_z", [P, R1, NB, D])
        relu_sum, ln_sum = sb("relu_sum", [P, R1, NB]), sb("ln_sum", [P, R1, NB])
        bcd_tok = sb("bcd_tok", [P, R1, 3, NB * N])
        bcd = sb("bcd", [Q, R1, 3, P])
        keep_h, drive, hs, hc = (sb(n, [Q, R1, P]) for n in ("keep_h", "drive", "hs", "hc"))
        s_tok = sb("s_tok", [P, R1, NB])
        x1p = sb("x1p", [P, R1, NB, D])
        stats, mv = sb("stats", [P, R1, NB, 6]), sb("mv", [P, R1, NB, 2])
        var_eps = sb("var_eps", [P, R1, NB])
        lg1, lg2, lg3 = (sb(n, [P, R1, NB, E]) for n in ("lg1", "lg2", "lg3"))
        rstd, nmr = sb("rstd", [P, TILES]), sb("nmr", [P, TILES])
        logits = sb("logits", [P, TILES, E])
        rows = sb("rows", [P, TILES, ROW])

        top, tmp_te, pick, onehot = sb("top", [P, TILES]), sb("tmp_te", [P, TILES, E]), sb("pick", [P, TILES]), sb("onehot", [P, TILES, E])
        cnt, cnt_in, first_row = (sb(n, [P, E, TILES]) for n in ("cnt", "cnt_in", "first_row"))
        tiles_i, tiles_f, tiles_in, tiles_ex = sb("tiles_i", [P, E], i32), sb("tiles_f", [P, E]), sb("tiles_in", [P, E]), sb("tiles_ex", [P, E])
        dest_f, dest = sb("dest_f", [P, TILES]), sb("dest", [P, TILES], i32)
        past = sb("past", [1, ST, E])
        expert_f, expert = sb("expert_f", [1, ST]), sb("expert", [1, ST], i32)
        rw_e, rw_t = sb("rw_e", [P, TILES]), sb("rw_t", [P, TILES])

        fr = sb("fr", [P, R2, ROW])
        fxt = sb("fxt", [P, 2, KC, P])
        silu_g, hid = sb("silu_g", [P, 2, F]), sb("hid", [P, 2, F])
        hidt = sb("hidt", [P, 2, P])
        x2p = sb("x2p", [P, 2, D])
        fst, fmv, fve, frs, fnm = sb("fst", [P, 2, 6]), sb("fmv", [P, 2, 2]), sb("fve", [P, 2]), sb("frs", [P, 2]), sb("fnm", [P, 2])
        fout = sb("fout", [P, R2, D])

        ps = ctx.enter_context(nc.psum_tensor("ps", [P, 8, 512], fp32))
        sorted_rows = nc.dram_tensor("sorted_rows", (ST * P, ROW), fp32).ap()
        token_col = D + 1

        setup_loaded, moe_loaded, bias_loaded = sem("setup_loaded"), sem("moe_loaded"), sem("bias_loaded")
        x_loaded, xt_loaded = [sem(f"x_loaded{i}") for i in range(R1)], [sem(f"xt_loaded{i}") for i in range(R1)]
        consts_ready, empty_ready, empty_stored = sem("consts_ready"), sem("empty_ready"), sem("empty_stored")
        setup_mm, setup_dve, setup_act = sem("setup_mm"), sem("setup_dve"), sem("setup_act")
        xh_ready, xl_ready, xbo_ready = sem("xh_ready"), sem("xl_ready"), sem("xbo_ready")
        z_ready, wo_ready, z_copied = sem("z_ready"), sem("wo_ready"), sem("z_copied")
        abs_ready, exp_ready, relu_dve, soft_ready = sem("abs_ready"), sem("exp_ready"), sem("relu_dve"), sem("soft_ready")
        delta_ready, bcd_ready, bcd_copied = sem("delta_ready"), sem("bcd_ready"), sem("bcd_copied")
        keep_ready, drive_ready, h_ready, hc_ready = sem("keep_ready"), sem("drive_ready"), sem("h_ready"), sem("hc_ready")
        s_ready, s_copied, x1p_ready, stats_ready, mv_ready = sem("s_ready"), sem("s_copied"), sem("x1p_ready"), sem("stats_ready"), sem("mv_ready")
        var_ready, rstd_ready, nmr_ready, norm_ready = sem("var_ready"), sem("rstd_ready"), sem("nmr_ready"), sem("norm_ready")
        lg1_ready, lg2_ready, lg3_ready, logits_ready = sem("lg1_ready"), sem("lg2_ready"), sem("lg3_ready"), sem("logits_ready")
        route_step, onehot_ready, ranks_ready = sem("route_step"), sem("onehot_ready"), sem("ranks_ready")
        top_ready, rw_exp_ready, rw_ready, dest_ready, expert_ready = sem("top_ready"), sem("rw_exp_ready"), sem("rw_ready"), sem("dest_ready"), sem("expert_ready")
        rows_scattered = sem("rows_scattered")
        fr_loaded = [sem(f"fr_loaded{i}") for i in range(R2)]
        fxt_ready, fxt_copied, gu_ready, silu_ready, hid_ready = sem("fxt_ready"), sem("fxt_copied"), sem("gu_ready"), sem("silu_ready"), sem("hid_ready")
        hidt_ready, hidt_copied, y_ready, x2p_ready, fst_ready, fmv_ready = sem("hidt_ready"), sem("hidt_copied"), sem("y_ready"), sem("x2p_ready"), sem("fst_ready"), sem("fmv_ready")
        fve_ready, frs_ready, fnm_ready, fout_ready = sem("fve_ready"), sem("frs_ready"), sem("fnm_ready"), sem("fout_ready")
        out_stored = [sem(f"out_stored{i}") for i in range(R2)]

        SETUP_LOADS = 11
        LOOP1 = (2, 6)
        LOOP2 = (R2 + 4, R2 + 4 + (ST - R2 - 4) // R2 * R2)
        x_v = x.rearrange("b (c p) d -> c p b d", p=P)

        block = ctx.enter_context(nc.Block())

        @block.sync
        def _(sp):
            def load_chunk(k):
                if not k.within(0, CH):
                    return
                wait(sp, xh_ready, k.n - 1)
                wait(sp, xl_ready, k.n - 1)
                wait(sp, xbo_ready, k.n - 1)
                sp.dma_start(xts[:, k.slot, :, :], xt[bass.ds(k.n, 1), :, :, :].rearrange("c p k t -> p (c k) t"))\
                  .then_inc(xt_loaded[k.slot], 16)
                sp.dma_start(xr[:, k.slot, :, :], x_v[bass.ds(k.n, 1), :, :, :].rearrange("c p b d -> p (c b) d"))\
                  .then_inc(x_loaded[k.slot], 16)

            load_chunk(Step(0, 0, R1))
            for kc in range(KC):
                sp.dma_start(wz[:, kc, 0:D], wd[kc * P:(kc + 1) * P, :]).then_inc(setup_loaded, 16)
            sp.dma_start(wo_f[:, :, :], wo.rearrange("(k p) n -> p k n", p=P)).then_inc(setup_loaded, 16)
            run_steps(sp, load_chunk, 1, *LOOP1, CH, R1)
            sp.dma_start(w_gu[:, :, :, :], wgu).then_inc(moe_loaded, 16)
            sp.dma_start(w_dn[:, :, :], wdn.rearrange("e f d -> f e d")).then_inc(moe_loaded, 16)

            sp.wait_ge(rows_scattered, 16 * TILES)

            def load_tile(j):
                if not j.within(0, ST):
                    return
                wait(sp, out_stored[j.slot], 16 * j.round)
                sp.dma_start(fr[:, j.slot, :], sorted_rows[bass.ds(j.n * P, P), :]).then_inc(fr_loaded[j.slot], 16)

            run_steps(sp, load_tile, 0, *LOOP2, ST, R2)
            for s in range(R2):
                sp.wait_ge(out_stored[s], 16 * len(range(s, ST, R2)))

        @block.scalar
        def _(act):
            act.preload_act_table_set("natural_log_exp_and_others")
            act.dma_start(wot_f[:, :, :], wot.rearrange("(k p) n -> p k n", p=P)).then_inc(setup_loaded, 16)
            act.dma_start(gwt_f[:, :, :], gwt.rearrange("(k p) n -> p k n", p=P)).then_inc(setup_loaded, 16)
            act.dma_start(bo_col[:, :], bo_cols).then_inc(setup_loaded, 16)
            act.dma_start(wz[:, :, D:D + N], wb.rearrange("(k p) n -> p k n", p=P)).then_inc(setup_loaded, 16)
            act.dma_start(wz[:, :, D + N:G0], wc.rearrange("(k p) n -> p k n", p=P)).then_inc(setup_loaded, 16)
            for kc in range(KC):
                act.dma_start(a4[:, kc, :, :], a_mat[kc * P:(kc + 1) * P, :].rearrange("p (a n) -> p a n", a=1).broadcast_to([P, NB, N]))\
                   .then_inc(setup_loaded, 16)
            for lo, hi, src in ((0, D, bd), (D, D + N, bb), (D + N, G0, bc)):
                act.dma_start(bias_f[0:2, lo:hi], src.rearrange("(a n) -> a n", a=1).broadcast_to([2, hi - lo])).then_inc(bias_loaded, 16)
            act.dma_start(bo_row[:, :], bo.rearrange("(a n) -> a n", a=1).broadcast_to([P, D])).then_inc(setup_loaded, 16)
            act.wait_ge(empty_ready, 2)
            act.dma_start(sorted_rows.rearrange("(t p) r -> p t r", p=P),
                          empty_row[:, :].rearrange("p (a r) -> p a r", a=1).broadcast_to([P, ST, ROW])).then_inc(empty_stored, 16)
            act.wait_ge(setup_mm, 3)
            act.activation(sig_a[:, 0:1], ps[0:Q, 7, 0:1], ACT.Exp, scale=-1.0 / D).then_inc(setup_act, 1)

            def copy_z(k, p):
                act.wait_ge(z_ready, k.n * NB + 2 * p + 2)
                wait(act, delta_ready, (k.n - 1) * 2)
                wait(act, logits_ready, k.n - 1)
                act.activation(zs[:, k.slot, 2 * p:2 * p + 2, :], ps[:, 0:2, 0:ZS], ACT.Copy).then_inc(z_copied, 1)

            def softplus(k, p):
                pair = az[:, k.slot, 2 * p:2 * p + 2, :]
                act.wait_ge(abs_ready, k.n * 2 + p + 1)
                act.activation(pair, pair, ACT.Exp, scale=-1.0).then_inc(exp_ready, 1)
                act.wait_ge(exp_ready, k.n * 2 + p + 1)
                b = 2 * p + 1
                act.activation(relu_z[:, k.slot, b, :], zs[:, k.slot, b, 0:D], ACT.Relu,
                               accum_out=relu_sum[:, k.slot, b:b + 1])
                for b in (2 * p, 2 * p + 1):
                    last = act.activation(az[:, k.slot, b, :], az[:, k.slot, b, :], ACT.Ln, bias=1.0,
                                          accum_out=ln_sum[:, k.slot, b:b + 1])
                last.then_inc(soft_ready, 1)

            def normalize(k):
                act.wait_ge(nmr_ready, k.n + 1)
                for b in range(NB):
                    tile = k.n * NB + b
                    act.activation(rows[:, bass.ds(tile, 1), 0:D].rearrange("p a d -> p (a d)"), x1p[:, k.slot, b, :], ACT.Identity,
                                   bias=nmr[:, bass.ds(tile, 1)], scale=rstd[:, bass.ds(tile, 1)]).then_inc(norm_ready, 1)

            def step(k):
                f = k.plus(1)
                front, back = f.within(0, CH), k.within(0, CH)
                if front:
                    copy_z(f, 0)
                if back:
                    act.wait_ge(bcd_ready, k.n + 1)
                    act.activation(bcd[:, k.slot, :, :], ps[0:Q, 6, 0:3 * P].rearrange("q (a t) -> q a t", a=3), ACT.Copy)\
                       .then_inc(bcd_copied, 1)
                if front:
                    softplus(f, 0)
                    copy_z(f, 1)
                if k.plus(-1).within(0, CH):
                    normalize(k.plus(-1))
                if front:
                    softplus(f, 1)

            run_steps(act, step, -1, *LOOP1, CH + 1, R1)
            act.wait_ge(top_ready, 1)
            act.activation(rw_e[:, :], rw_t[:, :], ACT.Exp, scale=-1.0).then_inc(rw_exp_ready, 1)

            act.preload_act_table_set("silu_and_others")

            def ffn_step(t):
                nxt, cur, prev, old = t.plus(1), t, t.plus(-1), t.plus(-3)
                if nxt.within(0, ST):
                    act.wait_ge(fxt_ready, nxt.n + 1)
                    wait(act, gu_ready, nxt.n - 1)
                    act.activation(fxt[:, nxt.c % 2, :, :], ps[:, 2 + nxt.c % 2, 0:D].rearrange("p (k t) -> p k t", k=KC), ACT.Copy)\
                       .then_inc(fxt_copied, 1)
                if prev.within(0, ST):
                    act.wait_ge(hidt_ready, prev.n + 1)
                    wait(act, y_ready, prev.n - 1)
                    act.activation(hidt[:, prev.c % 2, :], ps[:, 4 + prev.c % 2, 0:P], ACT.Copy).then_inc(hidt_copied, 1)
                if cur.within(0, ST):
                    act.wait_ge(gu_ready, cur.n + 1)
                    wait(act, hid_ready, cur.n - 1)
                    act.activation(silu_g[:, cur.c % 2, :], ps[:, cur.c % 2, 0:F], ACT.Silu, scale=fr[:, cur.slot, D:D + 1])\
                       .then_inc(silu_ready, 1)
                if old.within(0, ST):
                    act.wait_ge(fnm_ready, old.n + 1)
                    wait(act, out_stored[old.slot], 16 * old.round)
                    act.activation(fout[:, old.slot, :], x2p[:, old.c % 2, :], ACT.Identity, bias=fnm[:, old.c % 2:old.c % 2 + 1],
                                   scale=frs[:, old.c % 2:old.c % 2 + 1]).then_inc(fout_ready, 1)

            run_steps(act, ffn_step, -1, *LOOP2, ST + 3, R2)

        @block.gpsimd
        def _(pool):
            pool.memset(empty_row[:, :], 0.0).then_inc(empty_ready, 1)
            pool.wait_ge(empty_ready, 1)
            pool.memset(empty_row[:, token_col:token_col + 1].bitcast(i32), NO_TOKEN).then_inc(empty_ready, 1)
            pool.memset(ident[:, :], 0.0).then_inc(consts_ready, 1)
            pool.memset(ones[:, :], 1.0).then_inc(consts_ready, 1)
            pool.memset(below[:, :], 1.0).then_inc(consts_ready, 1)
            pool.memset(batch_sel[:, :], 1.0).then_inc(consts_ready, 1)
            pool.iota(falling_i[:, :], pattern=[[-1, E]], base=E, channel_multiplier=0).then_inc(consts_ready, 1)
            pool.iota(tile_no_i[:, :], pattern=[[1, ST]], base=0, channel_multiplier=0).then_inc(consts_ready, 1)
            pool.iota(rows[:, :, token_col:token_col + 1].bitcast(i32).rearrange("p (c b) a -> p c b a", b=NB),
                      pattern=[[P, CH], [T, NB], [1, 1]], base=0, channel_multiplier=1).then_inc(consts_ready, 1)
            pool.memset(minus_half[:, :], -0.5).then_inc(consts_ready, 1)
            pool.wait_ge(consts_ready, 8)
            pool.affine_select(out=ident[:, :], in_=ident[:, :], compare_op=ALU.not_equal, fill=1.0, base=0,
                               pattern=[[-1, P]], channel_multiplier=1).then_inc(consts_ready, 1)
            pool.affine_select(out=below[:, :], in_=below[:, :], compare_op=ALU.is_gt, fill=0.0, base=0,
                               pattern=[[1, P]], channel_multiplier=-1).then_inc(consts_ready, 1)
            pool.affine_select(out=batch_sel[:, :], in_=batch_sel[:, :], compare_op=ALU.is_ge, fill=0.0, base=0,
                               pattern=[[-N, NB]], channel_multiplier=1).then_inc(consts_ready, 1)
            pool.wait_ge(consts_ready, 11)
            pool.affine_select(out=batch_sel[:, :], in_=batch_sel[:, :], compare_op=ALU.is_ge, fill=0.0, base=N - 1,
                               pattern=[[N, NB]], channel_multiplier=-1).then_inc(consts_ready, 1)

            def step(k):
                f, ff, p1 = k.plus(1), k.plus(2), k.plus(-1)
                if p1.within(0, CH):
                    pool.wait_ge(var_ready, p1.n + 1)
                    pool.tensor_tensor(rstd[:, bass.ds(p1.n * NB, NB)], var_eps[:, p1.slot, :], minus_half[:, :], ALU.pow)\
                        .then_inc(rstd_ready, 1)
                    gates = zs[:, p1.slot, :, G0:G0 + E]
                    wo_gates = zs[:, p1.slot, :, G0 + E:ZS]

                    def spread(v):
                        return v.rearrange("p (b a) -> p b a", a=1).broadcast_to([P, NB, E])

                    pool.tensor_tensor(lg1[:, p1.slot, :, :], wo_gates, spread(s_tok[:, p1.slot, :]), ALU.mult).then_inc(lg1_ready, 1)
                    pool.tensor_tensor(lg3[:, p1.slot, :, :], gate_sum[:, :].rearrange("p (a e) -> p a e", a=1).broadcast_to([P, NB, E]),
                                       spread(mv[:, p1.slot, :, 0]), ALU.mult).then_inc(lg3_ready, 1)
                    pool.wait_ge(lg1_ready, p1.n + 1)
                    pool.tensor_tensor(lg2[:, p1.slot, :, :], lg1[:, p1.slot, :, :], gates, ALU.add).then_inc(lg2_ready, 1)
                    pool.wait_ge(lg3_ready, p1.n + 1)
                    pool.wait_ge(lg2_ready, p1.n + 1)
                    pool.tensor_tensor(logits[:, bass.ds(p1.n * NB, NB), :], lg2[:, p1.slot, :, :], lg3[:, p1.slot, :, :], ALU.subtract)\
                        .then_inc(logits_ready, 1)
                if f.within(0, CH):
                    pool.wait_ge(x_loaded[f.slot], 16 * (f.round + 1))
                    if isinstance(f.n, int) and f.n == 0:
                        pool.wait_ge(setup_loaded, 16 * SETUP_LOADS)
                    wait(pool, x1p_ready, (f.n - 1) * NB)
                    pool.tensor_tensor(xbo[:, f.slot, :, :], xr[:, f.slot, :, :],
                                       bo_row[:, :].rearrange("p (a d) -> p a d", a=1).broadcast_to([P, NB, D]), ALU.add)\
                        .then_inc(xbo_ready, 1)
                if ff.within(0, CH):
                    pool.wait_ge(xh_ready, ff.n + 1)
                    pool.tensor_tensor(xl[:, ff.slot, :, :], xts[:, ff.slot, :, :], xh[:, ff.slot, :, :].bitcast(fp32), ALU.subtract)\
                        .then_inc(xl_ready, 1)

            run_steps(pool, step, -2, *LOOP1, CH + 1, R1)

            pool.wait_ge(norm_ready, TILES)
            pool.wait_ge(rw_ready, 1)
            pool.wait_ge(dest_ready, 1)
            pool.wait_ge(empty_stored, 16)
            for t in range(TILES):
                pool.indirect_dma_start(sorted_rows[:, :], bass.IndirectOffsetOnAxis(dest[:, t:t + 1], axis=0), rows[:, t, :], None)\
                    .then_inc(rows_scattered, 16)

            def ffn_step(t):
                mid, old = t.plus(-2), t.plus(-4)
                if old.within(0, ST):
                    pool.wait_ge(fout_ready, old.n + 1)
                if mid.within(0, ST):
                    pool.wait_ge(fve_ready, mid.n + 1)
                    wait(pool, fout_ready, mid.n - 1)
                    pool.tensor_tensor(frs[:, mid.c % 2:mid.c % 2 + 1], fve[:, mid.c % 2:mid.c % 2 + 1], minus_half[:, 0:1], ALU.pow)\
                        .then_inc(frs_ready, 1)
                if old.within(0, ST):
                    pool.indirect_dma_start(out[:, :], bass.IndirectOffsetOnAxis(fr[:, old.slot, token_col:token_col + 1].bitcast(i32), axis=0),
                                            fout[:, old.slot, :], None, bounds_check=TOK - 1, oob_is_err=False)\
                        .then_inc(out_stored[old.slot], 16)

            run_steps(pool, ffn_step, 0, *LOOP2, ST + 4, R2)

        @block.vector
        def _(dve):
            linked = [0]

            def link(ins):
                linked[0] += 1
                ins.then_inc(route_step, 1)
                dve.wait_ge(route_step, linked[0])

            dve.memset(bias_hl[:, :].bitcast(fp32), 0.0).then_inc(setup_dve, 1)
            dve.memset(two_ones[:, :].bitcast(fp32), 0.0).then_inc(setup_dve, 1)
            dve.memset(keep[:, :, :], 1.0).then_inc(setup_dve, 1)
            dve.memset(hs[:, 1, :], 0.0).then_inc(setup_dve, 1)
            dve.wait_ge(setup_dve, 4)
            link(dve.memset(two_ones[0:2, :].bitcast(fp32), 1.0))
            link(dve.memset(keep[:, :, 0:1], 0.0))
            dve.wait_ge(consts_ready, 12)
            link(dve.tensor_copy(falling[:, :], falling_i[:, :]))
            link(dve.tensor_copy(tile_no[:, :], tile_no_i[:, :]))
            dve.wait_ge(setup_loaded, 16 * SETUP_LOADS)
            for kc in range(KC):
                ins = dve.tensor_scalar(bogw[:, kc, :], gwt_f[:, kc, :], bo_col[:, kc:kc + 1], None, ALU.mult)
                ins.then_inc(setup_dve, 1)
            dve.wait_ge(setup_mm, 1)
            link(dve.tensor_copy(wz[:, :, G0:G0 + E], gwt_f[:, :, :]))
            link(dve.tensor_copy(wz[:, :, G0 + E:ZS], ps[:, 0:KC, 0:E]))
            dve.wait_ge(setup_mm, 2)
            link(dve.tensor_copy(gate_sum[:, :], ps[:, 2, 0:E]))
            dve.wait_ge(bias_loaded, 48)
            link(dve.tensor_copy(bias_f[0:2, G0:G0 + E], ps[0:2, 3, 0:E]))
            link(dve.memset(bias_f[0:2, G0 + E:ZS], 0.0))
            link(dve.tensor_copy(wz_hi[:, :, :], wz[:, :, :]))
            link(dve.tensor_tensor(wz_lo[:, :, :], wz[:, :, :], wz_hi[:, :, :].bitcast(fp32), ALU.subtract))
            link(dve.tensor_copy(wo_hi[:, :, :], wo_f[:, :, :]))
            link(dve.tensor_tensor(wo_lo[:, :, :], wo_f[:, :, :], wo_hi[:, :, :].bitcast(fp32), ALU.subtract))
            link(dve.tensor_copy(bias_hl[0:2, :], bias_f[:, :]))
            link(dve.tensor_tensor(bias_hl[0:2, :], bias_f[:, :], bias_hl[0:2, :].bitcast(fp32), ALU.subtract))
            link(dve.tensor_copy(bias_hl[0:1, :], bias_f[0:1, :]))
            dve.wait_ge(setup_act, 1)
            link(dve.tensor_scalar_add(sig_a[:, 1:2], sig_a[:, 0:1], 1.0))
            link(dve.reciprocal(sig_a[:, 0:1], sig_a[:, 1:2]))
            dve.tensor_scalar(batch_sel[:, :], batch_sel[:, :], sig_a[:, 0:1], None, ALU.mult).then_inc(setup_dve, 1)

            def abs_relu(k, p):
                pair = zs[:, k.slot, 2 * p:2 * p + 2, 0:D]
                dve.wait_ge(z_copied, k.n * 2 + p + 1)
                dve.tensor_scalar(az[:, k.slot, 2 * p:2 * p + 2, :].bitcast(i32), pair.bitcast(i32), 0x7FFFFFFF, None, ALU.bitwise_and)\
                   .then_inc(abs_ready, 1)
                b = 2 * p
                dve.tensor_scalar(relu_z[:, k.slot, b, :], zs[:, k.slot, b, 0:D], 0.0, None, ALU.max, ALU.add,
                                  accum_out=relu_sum[:, k.slot, b:b + 1]).then_inc(relu_dve, 1)

            def split_hi(k):
                dve.wait_ge(xt_loaded[k.slot], 16 * (k.round + 1))
                wait(dve, wo_ready, (k.n - 1) * NB)
                dve.tensor_copy(xh[:, k.slot, :, :], xts[:, k.slot, :, :]).then_inc(xh_ready, 1)

            def scan(k):
                b_t, c_t, d_t = (bcd[:, k.slot, i, :] for i in range(3))
                dve.wait_ge(bcd_copied, k.n + 1)
                dve.tensor_scalar(keep_h[:, k.slot, :], d_t, -1.0 / D, 1.0, ALU.mult, ALU.add).then_inc(keep_ready, 1)
                dve.scalar_tensor_tensor(drive[:, k.slot, :], d_t, 1.0 / D, b_t, ALU.mult, ALU.mult).then_inc(drive_ready, 1)
                dve.wait_ge(keep_ready, k.n + 1)
                dve.wait_ge(drive_ready, k.n + 1)
                dve.tensor_tensor_scan(hs[:, k.slot, :], keep_h[:, k.slot, :], drive[:, k.slot, :],
                                       hs[:, 1 - k.slot, P - 1:P], ALU.mult, ALU.add).then_inc(h_ready, 1)
                dve.wait_ge(h_ready, k.n + 1)
                wait(dve, s_ready, k.n - 1)
                dve.tensor_tensor(hc[:, k.slot, :], hs[:, k.slot, :], c_t, ALU.mult).then_inc(hc_ready, 1)

            def residual_stats(k):
                dve.wait_ge(s_ready, k.n + 1)
                dve.tensor_copy(s_tok[:, k.slot, :], ps[:, 7, 0:NB]).then_inc(s_copied, 1)
                dve.wait_ge(s_copied, k.n + 1)
                dve.wait_ge(xbo_ready, k.n + 1)
                wait(dve, norm_ready, (k.n - 1) * NB)
                wait(dve, logits_ready, k.n - 1)
                for b in range(NB):
                    dve.wait_ge(wo_ready, k.n * NB + b // 2 * 2 + 2)
                    dve.scalar_tensor_tensor(x1p[:, k.slot, b, :], ps[:, 2 + 2 * k.slot + b // 2, b % 2 * D:(b % 2 + 1) * D],
                                             s_tok[:, k.slot, b:b + 1], xbo[:, k.slot, b, :], ALU.mult, ALU.add).then_inc(x1p_ready, 1)
                for b in range(NB):
                    dve.wait_ge(x1p_ready, k.n * NB + b + 1)
                    dve.bn_stats(stats[:, k.slot, b, :], x1p[:, k.slot, b, :]).then_inc(stats_ready, 1)

            def mean_var(k):
                for b in range(NB):
                    dve.bn_aggr(mv[:, k.slot, b, :], stats[:, k.slot, b, :]).then_inc(mv_ready, 1)
                dve.wait_ge(mv_ready, (k.n + 1) * NB)
                dve.tensor_scalar(var_eps[:, k.slot, :], mv[:, k.slot, :, 1], EPS, None, ALU.add).then_inc(var_ready, 1)

            def neg_mean_rstd(k):
                dve.wait_ge(rstd_ready, k.n + 1)
                dve.scalar_tensor_tensor(nmr[:, bass.ds(k.n * NB, NB)], mv[:, k.slot, :, 0], -1.0,
                                         rstd[:, bass.ds(k.n * NB, NB)], ALU.mult, ALU.mult).then_inc(nmr_ready, 1)

            def step(k):
                f, p1 = k.plus(1), k.plus(-1)
                front, back = f.within(0, CH), k.within(0, CH)
                if k.plus(2).within(0, CH):
                    split_hi(k.plus(2))
                if front:
                    abs_relu(f, 0)
                if back:
                    scan(k)
                if front:
                    abs_relu(f, 1)
                if p1.within(0, CH):
                    neg_mean_rstd(p1)
                if back:
                    residual_stats(k)
                if front:
                    wait(dve, bcd_ready, f.n - 1)
                    if back:
                        dve.wait_ge(stats_ready, (k.n + 1) * NB)
                    dve.tensor_copy(bcd_tok[:, f.slot, 0:2, :].rearrange("p c (b n) -> p c b n", n=N),
                                    zs[:, f.slot, :, D:G0].rearrange("p b (c n) -> p c b n", n=N)).then_inc(delta_ready, 1)
                elif back:
                    dve.wait_ge(stats_ready, (k.n + 1) * NB)
                if back:
                    mean_var(k)
                if front:
                    dve.wait_ge(soft_ready, (f.n + 1) * 2)
                    dve.wait_ge(relu_dve, (f.n + 1) * 2)
                    dve.tensor_tensor(bcd_tok[:, f.slot, 2, :].rearrange("p (b n) -> p b n", n=N),
                                      relu_sum[:, f.slot, :].rearrange("p (b a) -> p b a", a=1).broadcast_to([P, NB, N]),
                                      ln_sum[:, f.slot, :].rearrange("p (b a) -> p b a", a=1).broadcast_to([P, NB, N]),
                                      ALU.add).then_inc(delta_ready, 1)

            run_steps(dve, step, -2, *LOOP1, CH + 1, R1)

            def per_expert(v):
                return v.rearrange("p (t a) -> p t a", a=1).broadcast_to([P, TILES, E])

            falls = falling[:, :].rearrange("p (a e) -> p a e", a=1).broadcast_to([P, TILES, E])
            dve.wait_ge(logits_ready, CH)
            link(dve.reduce_max(top[:, :], logits[:, :, :], X_AXIS))
            dve.tensor_tensor(rw_t[:, :], top[:, :], rstd[:, :], ALU.mult).then_inc(top_ready, 1)
            link(dve.tensor_tensor(tmp_te[:, :, :], logits[:, :, :], per_expert(top[:, :]), ALU.is_ge))
            link(dve.tensor_tensor(tmp_te[:, :, :], tmp_te[:, :, :], falls, ALU.mult))
            link(dve.reduce_max(pick[:, :], tmp_te[:, :, :], X_AXIS))
            dve.tensor_tensor(onehot[:, :, :], falls, per_expert(pick[:, :]), ALU.is_equal).then_inc(onehot_ready, 1)
            dve.wait_ge(rw_exp_ready, 1)
            link(dve.tensor_scalar_add(rw_t[:, :], rw_e[:, :], 1.0))
            dve.reciprocal(rows[:, :, D], rw_t[:, :]).then_inc(rw_ready, 1)
            dve.wait_ge(ranks_ready, 2)
            link(dve.tensor_copy(cnt[:, :, :], ps[:, 1, 0:TILES * E].rearrange("p (t e) -> p e t", e=E)))
            flat = "p e t -> p (e t)"
            link(dve.tensor_tensor_scan(cnt_in[:, :, :].rearrange(flat), keep[:, :, :].rearrange(flat), cnt[:, :, :].rearrange(flat),
                                        0.0, ALU.mult, ALU.add))
            link(dve.tensor_scalar(tiles_i[:, :], cnt_in[:, :, TILES - 1], float(P - 1), None, ALU.add))
            link(dve.tensor_scalar(tiles_i[:, :], tiles_i[:, :], P.bit_length() - 1, None, ALU.logical_shift_right))
            link(dve.tensor_copy(tiles_f[:, :], tiles_i[:, :]))
            link(dve.tensor_tensor_scan(tiles_in[:, :], ones[:, 0:E], tiles_f[:, :], 0.0, ALU.mult, ALU.add))
            link(dve.tensor_tensor(tiles_ex[:, :], tiles_in[:, :], tiles_f[:, :], ALU.subtract))
            link(dve.tensor_tensor(cnt[:, :, :], cnt_in[:, :, :], cnt[:, :, :], ALU.subtract))
            link(dve.scalar_tensor_tensor(first_row[:, :, :], tiles_ex[:, :].rearrange("p (e a) -> p e a", a=1).broadcast_to([P, E, TILES]),
                                          float(P), cnt[:, :, :], ALU.mult, ALU.add))
            link(dve.tensor_tensor(tmp_te[:, :, :], ps[:, 0, 0:TILES * E].rearrange("p (t e) -> p t e", e=E),
                                   first_row[:, :, :].rearrange("p e t -> p t e"), ALU.add))
            link(dve.tensor_tensor(tmp_te[:, :, :], tmp_te[:, :, :], onehot[:, :, :], ALU.mult))
            link(dve.reduce_sum(dest_f[:, :], tmp_te[:, :, :], X_AXIS))
            dve.tensor_copy(dest[:, :], dest_f[:, :]).then_inc(dest_ready, 1)
            link(dve.tensor_tensor(past[:, :, :], tile_no[:, :].rearrange("p (t a) -> p t a", a=1).broadcast_to([1, ST, E]),
                                   tiles_in[0:1, :].rearrange("p (a e) -> p a e", a=1).broadcast_to([1, ST, E]), ALU.is_ge))
            link(dve.reduce_sum(expert_f[:, :], past[:, :, :], X_AXIS))
            dve.tensor_scalar(expert[:, :], expert_f[:, :], float(E - 1), None, ALU.min).then_inc(expert_ready, 1)

            def ffn_step(t):
                cur, mid, old = t, t.plus(-2), t.plus(-3)
                if cur.within(0, ST):
                    dve.wait_ge(silu_ready, cur.n + 1)
                    wait(dve, hidt_ready, cur.n - 1)
                    dve.scalar_tensor_tensor(hid[:, cur.c % 2, :], ps[:, cur.c % 2, F:2 * F], fr[:, cur.slot, D:D + 1],
                                             silu_g[:, cur.c % 2, :], ALU.mult, ALU.mult).then_inc(hid_ready, 1)
                if mid.within(0, ST):
                    h = mid.c % 2
                    dve.wait_ge(y_ready, mid.n + 1)
                    wait(dve, fout_ready, mid.n - 1)
                    dve.tensor_tensor(x2p[:, h, :], ps[:, 6 + h, 0:D], fr[:, mid.slot, 0:D], ALU.add).then_inc(x2p_ready, 1)
                    dve.wait_ge(x2p_ready, mid.n + 1)
                    dve.bn_stats(fst[:, h, :], x2p[:, h, :]).then_inc(fst_ready, 1)
                if old.within(0, ST):
                    h = old.c % 2
                    dve.wait_ge(frs_ready, old.n + 1)
                    if mid.within(0, ST):
                        dve.wait_ge(fst_ready, mid.n + 1)
                    dve.scalar_tensor_tensor(fnm[:, h:h + 1], fmv[:, h, 0:1], -1.0, frs[:, h:h + 1], ALU.mult, ALU.mult)\
                       .then_inc(fnm_ready, 1)
                if mid.within(0, ST):
                    h = mid.c % 2
                    if not old.within(0, ST):
                        dve.wait_ge(fst_ready, mid.n + 1)
                    dve.bn_aggr(fmv[:, h, :], fst[:, h, :]).then_inc(fmv_ready, 1)
                    dve.wait_ge(fmv_ready, mid.n + 1)
                    dve.tensor_scalar(fve[:, h:h + 1], fmv[:, h, 1:2], EPS, None, ALU.add).then_inc(fve_ready, 1)

            run_steps(dve, ffn_step, 0, *LOOP2, ST + 3, R2)

        @block.tensor
        def _(pe):
            pe.wait_ge(setup_loaded, 16 * SETUP_LOADS)
            pe.wait_ge(consts_ready, 12)
            for ic in range(KC):
                for jc in range(KC):
                    mm = pe.matmul(ps[:, ic, 0:E], wot_f[:, jc, ic * P:(ic + 1) * P], gwt_f[:, jc, :], start=(jc == 0), stop=(jc == KC - 1))
            mm.then_inc(setup_mm, 1)
            for jc in range(KC):
                pe.matmul(ps[:, 2, 0:E], ones[:, :], gwt_f[:, jc, :], start=(jc == 0), stop=(jc == KC - 1))
            pe.wait_ge(setup_dve, 6)
            for jc in range(KC):
                mm = pe.matmul(ps[:, 3, 0:E], ones[:, :], bogw[:, jc, :], start=(jc == 0), stop=(jc == KC - 1))
            mm.then_inc(setup_mm, 1)
            for jc in range(KC):
                mm = pe.matmul(ps[0:Q, 7, 0:1], a4[:, jc, :, :].rearrange("p b n -> p (b n)"), ones[:, 0:1], start=(jc == 0), stop=(jc == KC - 1))
            mm.then_inc(setup_mm, 1)
            pe.wait_ge(setup_dve, 7)

            def products(dst, k, b, w_hi, w_lo, bias):
                tok = slice(b * P, (b + 1) * P)
                terms = [(xh, w_hi), (xh, w_lo), (xl, w_hi)]
                if bias:
                    pe.matmul(dst, two_ones[:, :], bias_hl[:, :], start=True, stop=False)
                for i, (xs, w) in enumerate(terms):
                    for kc in range(KC):
                        mm = pe.matmul(dst, xs[:, k.slot, kc, tok], w[:, kc, :], start=(not bias and i == 0 and kc == 0),
                                       stop=(i == len(terms) - 1 and kc == KC - 1))
                return mm

            def tile_pair(k, p):
                if p == 0:
                    pe.wait_ge(xh_ready, k.n + 1)
                    pe.wait_ge(xl_ready, k.n + 1)
                    wait(pe, x1p_ready, (k.n - 1) * NB)
                for b in (2 * p, 2 * p + 1):
                    wait(pe, z_copied, k.n * 2 + p)
                    products(ps[:, b % 2, 0:ZS], k, b, wz_hi, wz_lo, True).then_inc(z_ready, 1)
                for b in (2 * p, 2 * p + 1):
                    products(ps[:, 2 + 2 * k.slot + p, b % 2 * D:(b % 2 + 1) * D], k, b, wo_hi, wo_lo, False).then_inc(wo_ready, 1)

            def step(k):
                f = k.plus(1)
                front, back = f.within(0, CH), k.within(0, CH)
                if front:
                    tile_pair(f, 0)
                if back:
                    pe.wait_ge(delta_ready, (k.n + 1) * 2)
                    wait(pe, bcd_copied, k.n)
                    pe.transpose(ps[:, 6, 0:P], bcd_tok[:, k.slot, 0:2, :].rearrange("p c q -> p (c q)"), ident[:, :])
                    for i in (1, 2):
                        tr = pe.transpose(ps[0:Q, 6, i * P:(i + 1) * P], bcd_tok[:, k.slot, i, :], ident[:, :])
                    tr.then_inc(bcd_ready, 1)
                if front:
                    tile_pair(f, 1)
                if back:
                    pe.wait_ge(hc_ready, k.n + 1)
                    wait(pe, s_copied, k.n)
                    pe.matmul(ps[:, 7, 0:NB], hc[:, k.slot, :], batch_sel[:, :], start=True, stop=True).then_inc(s_ready, 1)

            run_steps(pe, step, -1, *LOOP1, CH, R1)

            pe.wait_ge(onehot_ready, 1)
            flat = onehot[:, :, :].rearrange("p t e -> p (t e)")
            pe.matmul(ps[:, 0, 0:TILES * E], below[:, :], flat, start=True, stop=True).then_inc(ranks_ready, 1)
            pe.matmul(ps[:, 1, 0:TILES * E], ones[:, :], flat, start=True, stop=True).then_inc(ranks_ready, 1)

            pe.wait_ge(expert_ready, 1)
            pe.wait_ge(moe_loaded, 32)

            def ffn_step(t):
                cur, nxt, prev, old = t, t.plus(1), t.plus(-1), t.plus(-2)
                if cur.within(0, ST):
                    h = cur.c % 2
                    e = pe.value_load(expert[0:1, bass.ds(cur.n, 1)], min_val=0, max_val=E - 1)
                    pe.wait_ge(fxt_copied, cur.n + 1)
                    wait(pe, hid_ready, cur.n - 1)
                    for kc in range(KC):
                        mm = pe.matmul(ps[:, h, 0:2 * F], fxt[:, h, kc, :], w_gu[:, bass.ds(e, 1), kc, :].rearrange("p a n -> p (a n)"),
                                       start=(kc == 0), stop=(kc == KC - 1))
                    mm.then_inc(gu_ready, 1)
                if nxt.within(0, ST):
                    h = nxt.c % 2
                    pe.wait_ge(fr_loaded[nxt.slot], 16 * (nxt.round + 1))
                    wait(pe, fxt_copied, nxt.n - 1)
                    for kc in range(KC):
                        tr = pe.transpose(ps[:, 2 + h, kc * P:(kc + 1) * P], fr[:, nxt.slot, kc * P:(kc + 1) * P], ident[:, :])
                    tr.then_inc(fxt_ready, 1)
                if prev.within(0, ST):
                    h = prev.c % 2
                    pe.wait_ge(hid_ready, prev.n + 1)
                    wait(pe, hidt_copied, prev.n - 1)
                    pe.transpose(ps[:, 4 + h, 0:P], hid[:, h, :], ident[:, :]).then_inc(hidt_ready, 1)
                if old.within(0, ST):
                    h = old.c % 2
                    e = pe.value_load(expert[0:1, bass.ds(old.n, 1)], min_val=0, max_val=E - 1)
                    pe.wait_ge(hidt_copied, old.n + 1)
                    wait(pe, x2p_ready, old.n - 1)
                    pe.matmul(ps[:, 6 + h, 0:D], hidt[:, h, :], w_dn[:, bass.ds(e, 1), :].rearrange("p a n -> p (a n)"),
                              start=True, stop=True).then_inc(y_ready, 1)

            run_steps(pe, ffn_step, -1, *LOOP2, ST + 2, R2)


def kernel(**inputs):
    import numpy as _np
    import concourse.bacc as _bacc
    from concourse import mybir as _mybir
    from concourse.bass_utils import run_bass_kernel_spmd as _run

    i = {k.removeprefix("L0_"): _np.asarray(v) for k, v in inputs.items()}
    x = i["attn_x"]
    nb, t, d = x.shape
    p = 128
    n_exp, f, _ = i["ffn_w_gate"].shape
    xt = x.reshape(nb, t // p, p, d // p, p).transpose(1, 4, 3, 0, 2).reshape(t // p, p, d // p, nb * p)
    wgu = _np.stack([i["ffn_w_gate"], i["ffn_w_up"]], axis=1)
    wgu = wgu.reshape(n_exp, 2, f, d // p, p).transpose(4, 0, 3, 1, 2).reshape(p, n_exp, d // p, 2 * f)
    given = {
        "x": x, "xt": xt, "wd": i["attn_Wd"], "wb": i["attn_Wb"], "wc": i["attn_Wc"], "wo": i["attn_Wo"], "wot": i["attn_Wo"].T,
        "bd": i["attn_bd"], "bb": i["attn_bb"], "bc": i["attn_bc"], "bo": i["attn_bo"], "bo_cols": i["attn_bo"].reshape(d // p, p).T, "a_mat": i["attn_A"],
        "gwt": i["ffn_gate_w"].T, "wgu": wgu, "wdn": i["ffn_w_down"].transpose(0, 2, 1),
    }
    nc = _bacc.Bacc("TRN2", target_bir_lowering=False, num_devices=1)
    arrays, args = {}, {}
    for name, a in given.items():
        a = _np.ascontiguousarray(a)
        arrays[f"in_{name}"] = a
        args[name] = nc.dram_tensor(f"in_{name}", a.shape, _mybir.dt.from_np(a.dtype), kind="ExternalInput").ap()
    args["out"] = nc.dram_tensor("out", (nb * t, d), _mybir.dt.float32, kind="ExternalOutput").ap()
    ssm_attention_then_top1_moe(nc, **args)
    r = _run(nc, [arrays], core_ids=[0])
    return r.results[0]["out"].reshape(nb, t, d)
```

```python
import concourse.bass as bass
from concourse import mybir
from contextlib import ExitStack


class Step:

    def __init__(self, turn, c, ring):
        self.turn, self.c, self.ring = turn, c, ring
        self.n = turn * ring + c
        self.slot = c % ring
        self.round = turn + c // ring

    def plus(self, d):
        return Step(self.turn, self.c + d, self.ring)

    def within(self, lo, hi):
        return not isinstance(self.n, int) or lo <= self.n < hi


def run_steps(engine, body, first, loop_from, loop_to, last, ring):
    for n in range(first, loop_from):
        body(Step(0, n, ring))
    if loop_to > loop_from:
        with engine.Fori(0, (loop_to - loop_from) // ring) as turn:
            for u in range(ring):
                body(Step(turn, loop_from + u, ring))
    for n in range(loop_to, last):
        body(Step(0, n, ring))


def wait(engine, sem, value):
    if not isinstance(value, int) or value > 0:
        engine.wait_ge(sem, value)


def ssm_attention_then_top1_moe(nc: bass.Bass, x, xt, wd, wb, wc, wo, wot, bd, bb, bc, bo, bo_cols, a_mat, gwt, wgu, wdn, out):
    fp32, fp32r, i32 = mybir.dt.float32, mybir.dt.float32r, mybir.dt.int32
    ALU = mybir.AluOpType
    ACT = mybir.ActivationFunctionType
    X_AXIS = mybir.AxisListType.X

    P = 128
    NB, T, D = x.shape
    N = wb.shape[1]
    E = gwt.shape[1]
    F = wdn.shape[1]
    KC = D // P
    CH = T // P
    TILES = CH * NB
    TOK = NB * T
    Q = NB * N
    ZS = D + 2 * N + 2 * E
    G0 = D + 2 * N
    ROW = D + 2
    ST = TILES + E - 1
    EPS = 1e-5
    NO_TOKEN = 1 << 20
    REGION = TILES + 1
    R1, R2 = 2, 8
    R3 = 4
    RES_LAG, STD_LAG, LN_LAG, OUT_LAG = 4, 5, 6, 7

    ctx = ExitStack()
    with ctx:
        def sb(name, shape, dt=fp32):
            return ctx.enter_context(nc.sbuf_tensor(name, shape, dt))

        def sem(name):
            return ctx.enter_context(nc.semaphore(name))

        wz = sb("wz", [P, KC, ZS])
        wz_hi, wz_lo = sb("wz_hi", [P, KC, ZS], fp32r), sb("wz_lo", [P, KC, ZS], fp32r)
        wo_f = sb("wo_f", [P, KC, D])
        wo_hi, wo_lo = sb("wo_hi", [P, KC, D], fp32r), sb("wo_lo", [P, KC, D], fp32r)
        wot_f, gwt_f, bogw = sb("wot_f", [P, KC, D]), sb("gwt_f", [P, KC, E]), sb("bogw", [P, KC, E])
        bo_col = sb("bo_col", [P, KC])
        bo_row = sb("bo_row", [P, D])
        bias_f, bias_hl = sb("bias_f", [2, ZS]), sb("bias_hl", [P, ZS], fp32r)
        two_ones = sb("two_ones", [P, P], fp32r)
        a4 = sb("a4", [P, KC, NB, N])
        ident, ones, below = sb("ident", [P, P]), sb("ones", [P, P]), sb("below", [P, P])
        batch_sel = sb("batch_sel", [Q, NB])
        sig_a = sb("sig_a", [Q, 2])
        gate_sum = sb("gate_sum", [P, E])
        falling, region = sb("falling", [P, E]), sb("region", [P, E])
        falling_i, region_i = sb("falling_i", [P, E], i32), sb("region_i", [P, E], i32)
        tile_no, tile_no_i = sb("tile_no", [1, ST]), sb("tile_no_i", [1, ST], i32)
        minus_half = sb("minus_half", [P, NB])
        empty_row = sb("empty_row", [P, ROW])
        w_gu, w_dn = sb("w_gu", [P, E, KC, 2 * F]), sb("w_dn", [P, E, D])

        xr, xts = sb("xr", [P, R1, NB, D]), sb("xts", [P, R1, KC, NB * P])
        xh, xl = sb("xh", [P, R1, KC, NB * P], fp32r), sb("xl", [P, R1, KC, NB * P], fp32r)
        xbo = sb("xbo", [P, R1, NB, D])
        zs = sb("zs", [P, R1, NB, ZS])
        az = sb("az", [P, R1, NB, D])
        relu_z = sb("relu_z", [P, R1, NB, D])
        relu_sum, ln_sum = sb("relu_sum", [P, R1, NB]), sb("ln_sum", [P, R1, NB])
        bcd_tok = sb("bcd_tok", [P, R1, 3, NB * N])
        bcd = sb("bcd", [Q, R1, 3, P])
        keep_h, drive, hs, hc = (sb(n, [Q, R1, P]) for n in ("keep_h", "drive", "hs", "hc"))
        s_tok = sb("s_tok", [P, R1, NB])
        x1p = sb("x1p", [P, R1, NB, D])
        stats, mv = sb("stats", [P, R1, NB, 6]), sb("mv", [P, R1, NB, 2])
        var_eps = sb("var_eps", [P, R1, NB])
        lg1, lg2, lg3 = (sb(n, [P, R1, NB, E]) for n in ("lg1", "lg2", "lg3"))
        rstd, nmr = sb("rstd", [P, R1, NB]), sb("nmr", [P, R1, NB])
        logits = sb("logits", [P, R1, NB, E])
        rows = sb("rows", [P, R1, NB, ROW])

        top, pick, candidates = sb("top", [P, R1, NB]), sb("pick", [P, R1, NB]), sb("candidates", [P, R1, NB, E])
        picked = sb("picked", [P, R1, 1 + NB, E])
        place, dest_f, dest = sb("place", [P, R1, NB, E]), sb("dest_f", [P, R1, NB]), sb("dest", [P, R1, NB], i32)
        rw_t, rw_e, rw_1 = (sb(n, [P, R1, NB]) for n in ("rw_t", "rw_e", "rw_1"))
        ends_i, tiles_i, tiles_f, tiles_in, gap = (sb("ends_i", [P, E], i32), sb("tiles_i", [P, E], i32), sb("tiles_f", [P, E]),
                                                   sb("tiles_in", [P, E]), sb("gap", [P, E]))
        past, past_gap = sb("past", [1, ST, E]), sb("past_gap", [1, ST, E])
        expert_f, expert = sb("expert_f", [1, ST]), sb("expert", [1, ST], i32)
        source_f, source = sb("source_f", [1, ST]), sb("source", [1, ST], i32)

        fr = sb("fr", [P, R2, ROW])
        fxt = sb("fxt", [P, R3, KC, P])
        silu_g, hid = sb("silu_g", [P, 2, F]), sb("hid", [P, 2, F])
        hidt = sb("hidt", [P, 2, P])
        x2p = sb("x2p", [P, R3, D])
        fst, fmv, fve, frs, fnm = sb("fst", [P, R3, 6]), sb("fmv", [P, R3, 2]), sb("fve", [P, R3]), sb("frs", [P, R3]), sb("fnm", [P, R3])
        token = sb("token", [P, R2], i32)
        fout = sb("fout", [P, R2, D])

        ps = ctx.enter_context(nc.psum_tensor("ps", [P, 8, 512], fp32))
        sorted_rows = nc.dram_tensor("sorted_rows", ((E * REGION + 1) * P, ROW), fp32).ap()
        token_col = D + 1
        RANKS = 64

        wz_loaded, wo_loaded, gate_loaded, bias_loaded = sem("wz_loaded"), sem("wo_loaded"), sem("gate_loaded"), sem("bias_loaded")
        a_loaded, bo_loaded, moe_loaded = sem("a_loaded"), sem("bo_loaded"), sem("moe_loaded")
        x_loaded, xt_loaded = [sem(f"x_loaded{i}") for i in range(R1)], [sem(f"xt_loaded{i}") for i in range(R1)]
        consts_ready, empty_ready, empty_stored = sem("consts_ready"), sem("empty_ready"), sem("empty_stored")
        setup_mm, setup_dve, setup_act = sem("setup_mm"), sem("setup_dve"), sem("setup_act")
        xh_ready, xl_ready, xbo_ready = sem("xh_ready"), sem("xl_ready"), sem("xbo_ready")
        z_ready, wo_ready, z_copied = sem("z_ready"), sem("wo_ready"), sem("z_copied")
        abs_ready, exp_ready, soft_ready = sem("abs_ready"), sem("exp_ready"), sem("soft_ready")
        delta_ready, bcd_ready, bcd_copied = sem("delta_ready"), sem("bcd_ready"), sem("bcd_copied")
        keep_ready, drive_ready, h_ready, hc_ready = sem("keep_ready"), sem("drive_ready"), sem("h_ready"), sem("hc_ready")
        s_ready, s_copied, x1p_ready, stats_ready, mv_ready = sem("s_ready"), sem("s_copied"), sem("x1p_ready"), sem("stats_ready"), sem("mv_ready")
        var_ready, rstd_ready, nmr_ready, norm_ready = sem("var_ready"), sem("rstd_ready"), sem("nmr_ready"), sem("norm_ready")
        lg1_ready, lg2_ready, lg3_ready, logits_ready = sem("lg1_ready"), sem("lg2_ready"), sem("lg3_ready"), sem("logits_ready")
        route_step, top_ready, cand_ready, first_ready, pick_ready = sem("route_step"), sem("top_ready"), sem("cand_ready"), sem("first_ready"), sem("pick_ready")
        onehot_ready, earlier_ready, ranks_ready, place_ready, dest_f_ready, dest_ready = sem("onehot_ready"), sem("earlier_ready"), sem("ranks_ready"), sem("place_ready"), sem("dest_f_ready"), sem("dest_ready")
        rw_t_ready, rw_exp_ready, rw_1_ready, rw_ready, token_ready = sem("rw_t_ready"), sem("rw_exp_ready"), sem("rw_1_ready"), sem("rw_ready"), sem("token_ready")
        rows_scattered = [sem(f"rows_scattered{i}") for i in range(R1)]
        ends_ready, ends_i_ready, expert_ready, source_ready, pads_stored = sem("ends_ready"), sem("ends_i_ready"), sem("expert_ready"), sem("source_ready"), sem("pads_stored")
        fr_loaded = [sem(f"fr_loaded{i}") for i in range(R2)]
        fxt_ready, fxt_copied, gu_ready, silu_ready, hid_ready = sem("fxt_ready"), sem("fxt_copied"), sem("gu_ready"), sem("silu_ready"), sem("hid_ready")
        hidt_ready, hidt_copied, y_ready, x2p_ready, fst_ready, fmv_ready = sem("hidt_ready"), sem("hidt_copied"), sem("y_ready"), sem("x2p_ready"), sem("fst_ready"), sem("fmv_ready")
        tok_ready = sem("tok_ready")
        fve_ready, frs_ready, fnm_ready, fout_ready = sem("fve_ready"), sem("frs_ready"), sem("fnm_ready"), sem("fout_ready")
        out_stored = [sem(f"out_stored{i}") for i in range(R2)]

        LOOP1 = (4, 6)
        LOOP2 = (R2 + OUT_LAG, R2 + OUT_LAG + (ST - 1 - R2 - OUT_LAG) // R2 * R2)
        x_v = x.rearrange("b (c p) d -> c p b d", p=P)

        block = ctx.enter_context(nc.Block())

        @block.sync
        def _(sp):
            def load_xt(k):
                wait(sp, xh_ready, k.n - 1)
                wait(sp, xl_ready, k.n - 1)
                sp.dma_start(xts[:, k.slot, :, :], xt[bass.ds(k.n, 1), :, :, :].rearrange("c p k t -> p (c k) t"))\
                  .then_inc(xt_loaded[k.slot], 16)

            def load_x(k):
                wait(sp, xbo_ready, (k.n - 1) * 2)
                sp.dma_start(xr[:, k.slot, :, :], x_v[bass.ds(k.n, 1), :, :, :].rearrange("c p b d -> p (c b) d"))\
                  .then_inc(x_loaded[k.slot], 16)

            def load_moe(k):
                some = bass.ds(k.n * (E // CH), E // CH)
                sp.dma_start(w_gu[:, some, :, :], wgu[:, some, :, :]).then_inc(moe_loaded, 16)
                sp.dma_start(w_dn[:, some, :], wdn[some, :, :].rearrange("e f d -> f e d")).then_inc(moe_loaded, 16)

            def load_chunk(k):
                if k.within(0, CH):
                    load_xt(k)
                    load_x(k)
                load_moe(k.plus(-1))

            sp.dma_start(wz[:, :, 0:D], wd.rearrange("(k p) n -> p k n", p=P)).then_inc(wz_loaded, 16)
            load_xt(Step(0, 0, R1))
            sp.dma_start(wo_f[:, :, :], wo.rearrange("(k p) n -> p k n", p=P)).then_inc(wo_loaded, 16)
            load_x(Step(0, 0, R1))
            run_steps(sp, load_chunk, 1, *LOOP1, CH + 1, R1)

            sp.wait_ge(ends_i_ready, 1)
            for e in range(E):
                end = sp.value_load(ends_i[0:1, e:e + 1], min_val=0, max_val=E * REGION * P)
                sp.dma_start(sorted_rows[bass.ds(end, P), :], empty_row[:, :]).then_inc(pads_stored, 16)

            sp.wait_ge(source_ready, 1)
            sp.wait_ge(pads_stored, 16 * E)
            sp.wait_ge(empty_stored, 16)
            for s in range(R1):
                sp.wait_ge(rows_scattered[s], 16 * NB * CH // R1)

            def load_tile(j):
                if not j.within(0, ST):
                    return
                at = nc.s_assert_within(sp.value_load(source[0:1, bass.ds(j.n, 1)]), 0, E * REGION,
                                        skip_runtime_bounds_check_because="a sum of counts, cut off at the tile of empty rows")
                wait(sp, x2p_ready, j.n + 1 - R2)
                wait(sp, tok_ready, j.n + 1 - R2)
                sp.dma_start(fr[:, j.slot, :], sorted_rows.rearrange("(t p) r -> t p r", p=P)[bass.ds(at, 1), :, :].rearrange("t p r -> p (t r)"))\
                  .then_inc(fr_loaded[j.slot], 16)

            run_steps(sp, load_tile, 0, *LOOP2, ST, R2)
            for s in range(R2):
                sp.wait_ge(out_stored[s], 16 * len(range(s, ST, R2)))

        @block.scalar
        def _(act):
            act.preload_act_table_set("natural_log_exp_and_others")
            act.dma_start(wot_f[:, :, :], wot.rearrange("(k p) n -> p k n", p=P)).then_inc(gate_loaded, 16)
            act.dma_start(gwt_f[:, :, :], gwt.rearrange("(k p) n -> p k n", p=P)).then_inc(gate_loaded, 16)
            act.dma_start(bo_col[:, :], bo_cols).then_inc(gate_loaded, 16)
            act.dma_start(wz[:, :, D:D + N], wb.rearrange("(k p) n -> p k n", p=P)).then_inc(wz_loaded, 16)
            act.dma_start(wz[:, :, D + N:G0], wc.rearrange("(k p) n -> p k n", p=P)).then_inc(wz_loaded, 16)
            for lo, hi, src in ((0, D, bd), (D, D + N, bb), (D + N, G0, bc)):
                act.dma_start(bias_f[0:2, lo:hi], src.rearrange("(a n) -> a n", a=1).broadcast_to([2, hi - lo])).then_inc(bias_loaded, 16)
            for kc in range(KC):
                act.dma_start(a4[:, kc, :, :], a_mat[kc * P:(kc + 1) * P, :].rearrange("p (a n) -> p a n", a=1).broadcast_to([P, NB, N]))\
                   .then_inc(a_loaded, 16)
            act.dma_start(bo_row[:, :], bo.rearrange("(a n) -> a n", a=1).broadcast_to([P, D])).then_inc(bo_loaded, 16)
            act.wait_ge(empty_ready, 2)
            act.dma_start(sorted_rows[E * REGION * P:(E * REGION + 1) * P, :], empty_row[:, :]).then_inc(empty_stored, 16)
            act.wait_ge(setup_mm, 3)
            act.activation(sig_a[:, 0:1], ps[0:Q, 7, 0:1], ACT.Exp, scale=-1.0 / D).then_inc(setup_act, 1)

            def copy_z(k, p):
                act.wait_ge(z_ready, k.n * NB + 2 * p + 2)
                wait(act, delta_ready, (k.n - 1) * 2)
                wait(act, lg2_ready, k.n - 1)
                act.activation(zs[:, k.slot, 2 * p:2 * p + 2, :], ps[:, 0:2, 0:ZS], ACT.Copy).then_inc(z_copied, 1)

            def softplus(k, p):
                pair = az[:, k.slot, 2 * p:2 * p + 2, :]
                act.wait_ge(abs_ready, k.n * 2 + p + 1)
                act.activation(pair, pair, ACT.Exp, scale=-1.0).then_inc(exp_ready, 1)
                for b in (2 * p, 2 * p + 1):
                    act.activation(relu_z[:, k.slot, b, :], zs[:, k.slot, b, 0:D], ACT.Relu, accum_out=relu_sum[:, k.slot, b:b + 1])
                act.wait_ge(exp_ready, k.n * 2 + p + 1)
                for b in (2 * p, 2 * p + 1):
                    last = act.activation(az[:, k.slot, b, :], az[:, k.slot, b, :], ACT.Ln, bias=1.0,
                                          accum_out=ln_sum[:, k.slot, b:b + 1])
                last.then_inc(soft_ready, 1)

            def normalize(k):
                act.wait_ge(nmr_ready, k.n + 1)
                wait(act, rows_scattered[k.slot], 16 * NB * k.round)
                for b in range(NB):
                    act.activation(rows[:, k.slot, b, 0:D], x1p[:, k.slot, b, :], ACT.Identity,
                                   bias=nmr[:, k.slot, b:b + 1], scale=rstd[:, k.slot, b:b + 1]).then_inc(norm_ready, 1)

            def router_exp(k):
                act.wait_ge(rw_t_ready, k.n + 1)
                wait(act, rw_1_ready, k.n - 1)
                act.activation(rw_e[:, k.slot, :], rw_t[:, k.slot, :], ACT.Exp, scale=-1.0).then_inc(rw_exp_ready, 1)

            def step(k):
                f, ff, p1 = k.plus(1), k.plus(2), k.plus(-1)
                if k.within(0, CH):
                    act.wait_ge(bcd_ready, k.n + 1)
                    act.activation(bcd[:, k.slot, :, :], ps[0:Q, 6, 0:3 * P].rearrange("q (a t) -> q a t", a=3), ACT.Copy)\
                       .then_inc(bcd_copied, 1)
                if f.within(0, CH):
                    softplus(f, 0)
                    copy_z(f, 1)
                if p1.within(0, CH):
                    normalize(p1)
                if f.within(0, CH):
                    softplus(f, 1)
                if ff.within(0, CH):
                    copy_z(ff, 0)
                if p1.within(0, CH):
                    router_exp(p1)

            run_steps(act, step, -2, *LOOP1, CH + 1, R1)

            act.preload_act_table_set("silu_and_others")

            def ffn_step(t):
                nxt, cur, prev, old = t.plus(1), t, t.plus(-2), t.plus(-LN_LAG)
                if nxt.within(0, ST):
                    act.wait_ge(fxt_ready, nxt.n + 1)
                    wait(act, gu_ready, nxt.n + 1 - R3)
                    act.activation(fxt[:, nxt.c % R3, :, :], ps[:, 2 + nxt.c % 2, 0:D].rearrange("p (k t) -> p k t", k=KC), ACT.Copy)\
                       .then_inc(fxt_copied, 1)
                if prev.within(0, ST):
                    act.wait_ge(hidt_ready, prev.n + 1)
                    wait(act, y_ready, prev.n - 1)
                    act.activation(hidt[:, prev.c % 2, :], ps[:, 4 + prev.c % 2, 0:P], ACT.Copy).then_inc(hidt_copied, 1)
                if old.within(0, ST):
                    r = old.c % R3
                    act.wait_ge(fnm_ready, old.n + 1)
                    wait(act, out_stored[old.slot], 16 * old.round)
                    act.activation(fout[:, old.slot, :], x2p[:, r, :], ACT.Identity, bias=fnm[:, r:r + 1],
                                   scale=frs[:, r:r + 1]).then_inc(fout_ready, 1)
                if cur.within(0, ST):
                    act.wait_ge(gu_ready, cur.n + 1)
                    wait(act, hid_ready, cur.n - 1)
                    act.activation(silu_g[:, cur.c % 2, :], ps[:, cur.c % 2, 0:F], ACT.Silu, scale=fr[:, cur.slot, D:D + 1])\
                       .then_inc(silu_ready, 1)

            run_steps(act, ffn_step, -1, *LOOP2, ST + LN_LAG, R2)

        @block.gpsimd
        def _(pool):
            pool.memset(empty_row[:, :], 0.0).then_inc(empty_ready, 1)
            pool.wait_ge(empty_ready, 1)
            pool.memset(empty_row[:, token_col:token_col + 1].bitcast(i32), NO_TOKEN).then_inc(empty_ready, 1)
            pool.memset(ident[:, :], 0.0).then_inc(consts_ready, 1)
            pool.memset(ones[:, :], 1.0).then_inc(consts_ready, 1)
            pool.memset(below[:, :], 1.0).then_inc(consts_ready, 1)
            pool.memset(batch_sel[:, :], 1.0).then_inc(consts_ready, 1)
            pool.iota(falling_i[:, :], pattern=[[-1, E]], base=E, channel_multiplier=0).then_inc(consts_ready, 1)
            pool.iota(region_i[:, :], pattern=[[REGION, E]], base=0, channel_multiplier=0).then_inc(consts_ready, 1)
            pool.iota(tile_no_i[:, :], pattern=[[1, ST]], base=0, channel_multiplier=0).then_inc(consts_ready, 1)
            pool.iota(rows[:, :, :, token_col:token_col + 1].bitcast(i32),
                      pattern=[[P, R1], [T, NB], [1, 1]], base=-R1 * P, channel_multiplier=1).then_inc(consts_ready, 1)
            pool.memset(minus_half[:, :], -0.5).then_inc(consts_ready, 1)
            pool.wait_ge(consts_ready, 9)
            pool.affine_select(out=ident[:, :], in_=ident[:, :], compare_op=ALU.not_equal, fill=1.0, base=0,
                               pattern=[[-1, P]], channel_multiplier=1).then_inc(consts_ready, 1)
            pool.affine_select(out=below[:, :], in_=below[:, :], compare_op=ALU.is_gt, fill=0.0, base=0,
                               pattern=[[1, P]], channel_multiplier=-1).then_inc(consts_ready, 1)
            pool.affine_select(out=batch_sel[:, :], in_=batch_sel[:, :], compare_op=ALU.is_ge, fill=0.0, base=0,
                               pattern=[[-N, NB]], channel_multiplier=1).then_inc(consts_ready, 1)
            pool.wait_ge(consts_ready, 12)
            pool.affine_select(out=batch_sel[:, :], in_=batch_sel[:, :], compare_op=ALU.is_ge, fill=0.0, base=N - 1,
                               pattern=[[N, NB]], channel_multiplier=-1).then_inc(consts_ready, 1)

            def spread(v):
                return v.rearrange("p (b a) -> p b a", a=1).broadcast_to([P, NB, E])

            def step(k):
                f, p1, p2 = k.plus(1), k.plus(-1), k.plus(-2)
                if p1.within(0, CH):
                    pool.wait_ge(var_ready, p1.n + 1)
                    wait(pool, norm_ready, (p1.n - 1) * NB)
                    wait(pool, rw_t_ready, p1.n - 1)
                    wait(pool, cand_ready, p1.n - 1)
                    pool.tensor_tensor(rstd[:, p1.slot, :], var_eps[:, p1.slot, :], minus_half[:, :], ALU.pow)\
                        .then_inc(rstd_ready, 1)
                    pool.tensor_tensor(lg3[:, p1.slot, :, :], gate_sum[:, :].rearrange("p (a e) -> p a e", a=1).broadcast_to([P, NB, E]),
                                       spread(mv[:, p1.slot, :, 0]), ALU.mult).then_inc(lg3_ready, 1)
                    pool.wait_ge(lg3_ready, p1.n + 1)
                    pool.wait_ge(lg2_ready, p1.n + 1)
                    pool.tensor_tensor(logits[:, p1.slot, :, :], lg2[:, p1.slot, :, :], lg3[:, p1.slot, :, :], ALU.subtract)\
                        .then_inc(logits_ready, 1)

                def add_bo(lo, hi):
                    pool.tensor_tensor(xbo[:, f.slot, lo:hi, :], xr[:, f.slot, lo:hi, :],
                                       bo_row[:, :].rearrange("p (a d) -> p a d", a=1).broadcast_to([P, hi - lo, D]), ALU.add)\
                        .then_inc(xbo_ready, 1)

                if f.within(0, CH):
                    pool.wait_ge(x_loaded[f.slot], 16 * (f.round + 1))
                    if isinstance(f.n, int) and f.n == 0:
                        pool.wait_ge(bo_loaded, 16)
                    wait(pool, x1p_ready, (f.n - 1) * NB)
                    add_bo(0, NB // 2)
                if k.within(0, CH):
                    pool.wait_ge(s_copied, k.n + 1)
                    pool.wait_ge(z_copied, (k.n + 1) * 2)
                    wait(pool, lg2_ready, k.n)
                    pool.tensor_tensor(lg1[:, k.slot, :, :], zs[:, k.slot, :, G0 + E:ZS], spread(s_tok[:, k.slot, :]), ALU.mult).then_inc(lg1_ready, 1)
                    pool.wait_ge(lg1_ready, k.n + 1)
                    wait(pool, logits_ready, k.n - 1)
                    pool.tensor_tensor(lg2[:, k.slot, :, :], lg1[:, k.slot, :, :], zs[:, k.slot, :, G0:G0 + E], ALU.add).then_inc(lg2_ready, 1)
                if p2.within(0, CH):
                    pool.wait_ge(norm_ready, (p2.n + 1) * NB)
                    pool.wait_ge(rw_ready, p2.n + 1)
                    wait(pool, token_ready, p2.n + 1)
                    pool.wait_ge(dest_ready, p2.n + 1)
                if f.within(0, CH):
                    add_bo(NB // 2, NB)
                if p2.within(0, CH):
                    for b in range(NB):
                        pool.indirect_dma_start(sorted_rows[:, :], bass.IndirectOffsetOnAxis(dest[:, p2.slot, b:b + 1], axis=0),
                                                rows[:, p2.slot, b, :], None).then_inc(rows_scattered[p2.slot], 16)

            run_steps(pool, step, -1, *LOOP1, CH + 2, R1)

            def ffn_step(t):
                std, old = t.plus(-STD_LAG), t.plus(-OUT_LAG)
                if old.within(0, ST):
                    pool.wait_ge(fout_ready, old.n + 1)
                    pool.wait_ge(tok_ready, old.n + 1)
                if std.within(0, ST):
                    r = std.c % R3
                    pool.wait_ge(fve_ready, std.n + 1)
                    wait(pool, fout_ready, std.n + 1 - R3)
                    pool.tensor_tensor(frs[:, r:r + 1], fve[:, r:r + 1], minus_half[:, 0:1], ALU.pow).then_inc(frs_ready, 1)
                if old.within(0, ST):
                    pool.indirect_dma_start(out[:, :], bass.IndirectOffsetOnAxis(token[:, old.slot:old.slot + 1], axis=0),
                                            fout[:, old.slot, :], None, bounds_check=TOK - 1, oob_is_err=False)\
                        .then_inc(out_stored[old.slot], 16)

            run_steps(pool, ffn_step, STD_LAG, *LOOP2, ST + OUT_LAG, R2)

        @block.vector
        def _(dve):
            linked = [0]

            def link(ins):
                linked[0] += 1
                ins.then_inc(route_step, 1)
                dve.wait_ge(route_step, linked[0])

            dve.memset(bias_hl[:, :].bitcast(fp32), 0.0).then_inc(setup_dve, 1)
            dve.memset(two_ones[:, :].bitcast(fp32), 0.0).then_inc(setup_dve, 1)
            dve.memset(hs[:, 1, :], 0.0).then_inc(setup_dve, 1)
            dve.wait_ge(setup_dve, 3)
            link(dve.memset(two_ones[0:2, :].bitcast(fp32), 1.0))
            dve.wait_ge(consts_ready, 13)
            link(dve.tensor_copy(falling[:, :], falling_i[:, :]))
            link(dve.tensor_copy(tile_no[:, :], tile_no_i[:, :]))
            link(dve.tensor_copy(region[:, :], region_i[:, :]))
            link(dve.tensor_copy(picked[:, 0, 0, :], region[:, :]))
            def split_hi(k):
                dve.wait_ge(xt_loaded[k.slot], 16 * (k.round + 1))
                wait(dve, wo_ready, (k.n - 1) * NB)
                dve.tensor_copy(xh[:, k.slot, :, :], xts[:, k.slot, :, :]).then_inc(xh_ready, 1)

            def split_lo(k):
                dve.wait_ge(xh_ready, k.n + 1)
                dve.tensor_tensor(xl[:, k.slot, :, :], xts[:, k.slot, :, :], xh[:, k.slot, :, :].bitcast(fp32), ALU.subtract)\
                   .then_inc(xl_ready, 1)

            def split_weights(hi, lo, w):
                link(dve.tensor_copy(hi, w))
                dve.tensor_tensor(lo, w, hi.bitcast(fp32), ALU.subtract).then_inc(setup_dve, 1)

            dve.wait_ge(gate_loaded, 48)
            for kc in range(KC):
                ins = dve.tensor_scalar(bogw[:, kc, :], gwt_f[:, kc, :], bo_col[:, kc:kc + 1], None, ALU.mult)
                ins.then_inc(setup_dve, 1)

            split_hi(Step(0, 0, R1))
            dve.wait_ge(wz_loaded, 48)
            split_weights(wz_hi[:, :, 0:G0], wz_lo[:, :, 0:G0], wz[:, :, 0:G0])
            split_lo(Step(0, 0, R1))
            dve.wait_ge(setup_mm, 2)
            dve.wait_ge(bias_loaded, 48)
            dve.memset(bias_f[0:2, G0 + E:ZS], 0.0).then_inc(setup_dve, 1)
            dve.tensor_copy(wz[:, :, G0:G0 + E], gwt_f[:, :, :]).then_inc(setup_dve, 1)
            dve.tensor_copy(gate_sum[:, :], ps[:, 2, 0:E]).then_inc(setup_dve, 1)
            dve.tensor_copy(bias_f[0:2, G0:G0 + E], ps[0:2, 3, 0:E]).then_inc(setup_dve, 1)
            link(dve.tensor_copy(wz[:, :, G0 + E:ZS], ps[:, 0:KC, 0:E]))
            dve.wait_ge(setup_dve, 10)
            split_weights(wz_hi[:, :, G0:ZS], wz_lo[:, :, G0:ZS], wz[:, :, G0:ZS])
            link(dve.tensor_copy(bias_hl[0:2, :], bias_f[:, :]))
            link(dve.tensor_tensor(bias_hl[0:2, :], bias_f[:, :], bias_hl[0:2, :].bitcast(fp32), ALU.subtract))
            dve.tensor_copy(bias_hl[0:1, :], bias_f[0:1, :]).then_inc(setup_dve, 1)
            dve.wait_ge(wo_loaded, 16)
            split_weights(wo_hi[:, :, :], wo_lo[:, :, :], wo_f[:, :, :])
            dve.wait_ge(setup_act, 1)
            link(dve.tensor_scalar_add(sig_a[:, 1:2], sig_a[:, 0:1], 1.0))
            link(dve.reciprocal(sig_a[:, 0:1], sig_a[:, 1:2]))
            dve.tensor_scalar(batch_sel[:, :], batch_sel[:, :], sig_a[:, 0:1], None, ALU.mult).then_inc(setup_dve, 1)

            def abs_z(k, p):
                pair = zs[:, k.slot, 2 * p:2 * p + 2, 0:D]
                dve.wait_ge(z_copied, k.n * 2 + p + 1)
                dve.tensor_scalar(az[:, k.slot, 2 * p:2 * p + 2, :].bitcast(i32), pair.bitcast(i32), 0x7FFFFFFF, None, ALU.bitwise_and)\
                   .then_inc(abs_ready, 1)

            def scan(k):
                b_t, c_t, d_t = (bcd[:, k.slot, i, :] for i in range(3))
                dve.wait_ge(bcd_copied, k.n + 1)
                dve.tensor_scalar(keep_h[:, k.slot, :], d_t, -1.0 / D, 1.0, ALU.mult, ALU.add).then_inc(keep_ready, 1)
                dve.scalar_tensor_tensor(drive[:, k.slot, :], d_t, 1.0 / D, b_t, ALU.mult, ALU.mult).then_inc(drive_ready, 1)
                dve.wait_ge(keep_ready, k.n + 1)
                dve.wait_ge(drive_ready, k.n + 1)
                dve.tensor_tensor_scan(hs[:, k.slot, :], keep_h[:, k.slot, :], drive[:, k.slot, :],
                                       hs[:, 1 - k.slot, P - 1:P], ALU.mult, ALU.add).then_inc(h_ready, 1)
                dve.wait_ge(h_ready, k.n + 1)
                wait(dve, s_ready, k.n - 1)
                dve.tensor_tensor(hc[:, k.slot, :], hs[:, k.slot, :], c_t, ALU.mult).then_inc(hc_ready, 1)

            def residual_stats(k):
                dve.wait_ge(s_ready, k.n + 1)
                dve.tensor_copy(s_tok[:, k.slot, :], ps[:, 7, 0:NB]).then_inc(s_copied, 1)
                dve.wait_ge(s_copied, k.n + 1)
                dve.wait_ge(xbo_ready, (k.n + 1) * 2)
                wait(dve, norm_ready, (k.n - 1) * NB)
                wait(dve, logits_ready, k.n - 1)
                routing = route(k.plus(-1)) if k.plus(-1).within(0, CH) else [lambda: None] * NB
                for b in range(NB):
                    dve.wait_ge(wo_ready, k.n * NB + b // 2 * 2 + 2)
                    dve.scalar_tensor_tensor(x1p[:, k.slot, b, :], ps[:, 2 + 2 * k.slot + b // 2, b % 2 * D:(b % 2 + 1) * D],
                                             s_tok[:, k.slot, b:b + 1], xbo[:, k.slot, b, :], ALU.mult, ALU.add).then_inc(x1p_ready, 1)
                    routing[b]()
                for b in range(NB):
                    dve.wait_ge(x1p_ready, k.n * NB + b + 1)
                    dve.bn_stats(stats[:, k.slot, b, :], x1p[:, k.slot, b, :]).then_inc(stats_ready, 1)

            def mean_var(k):
                for b in range(NB):
                    dve.bn_aggr(mv[:, k.slot, b, :], stats[:, k.slot, b, :]).then_inc(mv_ready, 1)
                dve.wait_ge(mv_ready, (k.n + 1) * NB)
                dve.tensor_scalar(var_eps[:, k.slot, :], mv[:, k.slot, :, 1], EPS, None, ALU.add).then_inc(var_ready, 1)

            def neg_mean_rstd(k):
                dve.wait_ge(rstd_ready, k.n + 1)
                dve.scalar_tensor_tensor(nmr[:, k.slot, :], mv[:, k.slot, :, 0], -1.0, rstd[:, k.slot, :], ALU.mult, ALU.mult)\
                   .then_inc(nmr_ready, 1)

            falls = falling[:, :].rearrange("p (a e) -> p a e", a=1).broadcast_to([P, NB, E])

            def per_expert(v):
                return v.rearrange("p (b a) -> p b a", a=1).broadcast_to([P, NB, E])

            def route_top(k):
                dve.wait_ge(logits_ready, k.n + 1)
                dve.reduce_max(top[:, k.slot, :], logits[:, k.slot, :, :], X_AXIS).then_inc(top_ready, 1)

            def route_cand(k):
                dve.wait_ge(top_ready, k.n + 1)
                dve.tensor_tensor(rw_t[:, k.slot, :], top[:, k.slot, :], rstd[:, k.slot, :], ALU.mult).then_inc(rw_t_ready, 1)
                dve.tensor_tensor(candidates[:, k.slot, :, :], logits[:, k.slot, :, :], per_expert(top[:, k.slot, :]), ALU.is_ge)\
                   .then_inc(cand_ready, 1)

            def route_first(k):
                dve.wait_ge(cand_ready, k.n + 1)
                dve.tensor_tensor(candidates[:, k.slot, :, :], candidates[:, k.slot, :, :], falls, ALU.mult).then_inc(first_ready, 1)

            def route_pick(k):
                dve.wait_ge(first_ready, k.n + 1)
                dve.reduce_max(pick[:, k.slot, :], candidates[:, k.slot, :, :], X_AXIS).then_inc(pick_ready, 1)

            def route_onehot(k):
                dve.wait_ge(pick_ready, k.n + 1)
                wait(dve, ranks_ready, k.n - 1)
                wait(dve, place_ready, k.n - 1)
                dve.tensor_tensor(picked[:, k.slot, 1:1 + NB, :], falls, per_expert(pick[:, k.slot, :]), ALU.is_equal).then_inc(onehot_ready, 1)

            def route(k):
                return [lambda: route_cand(k), lambda: route_first(k), lambda: route_pick(k), lambda: route_onehot(k)]

            def route_earlier(k):
                dve.wait_ge(onehot_ready, k.n + 1)
                wait(dve, ranks_ready, k.n)
                dve.reduce_sum(picked[:, 1 - k.slot, 0, :], picked[:, k.slot, :, :].rearrange("p b e -> p e b"), X_AXIS).then_inc(earlier_ready, 1)

            def router_weight_1(k):
                dve.wait_ge(rw_exp_ready, k.n + 1)
                dve.tensor_scalar_add(rw_1[:, k.slot, :], rw_e[:, k.slot, :], 1.0).then_inc(rw_1_ready, 1)

            def router_weight(k):
                dve.wait_ge(rw_1_ready, k.n + 1)
                wait(dve, rows_scattered[k.slot], 16 * NB * k.round)
                dve.reciprocal(rows[:, k.slot, :, D], rw_1[:, k.slot, :]).then_inc(rw_ready, 1)
                numbers = rows[:, k.slot, :, token_col].bitcast(i32)
                dve.tensor_scalar(numbers, numbers, R1 * P, None, ALU.add).then_inc(token_ready, 1)

            def places(k):
                dve.wait_ge(ranks_ready, k.n + 1)
                wait(dve, dest_f_ready, k.n)
                dve.tensor_tensor(place[:, k.slot, :, :], ps[:, 7, RANKS:RANKS + NB * E].rearrange("p (b e) -> p b e", e=E),
                                  picked[:, k.slot, 1:1 + NB, :], ALU.mult).then_inc(place_ready, 1)

            def destinations(k):
                dve.wait_ge(place_ready, k.n + 1)
                dve.reduce_sum(dest_f[:, k.slot, :], place[:, k.slot, :, :], X_AXIS).then_inc(dest_f_ready, 1)

            def integer_destinations(k):
                dve.wait_ge(dest_f_ready, k.n + 1)
                wait(dve, rows_scattered[k.slot], 16 * NB * k.round)
                dve.tensor_copy(dest[:, k.slot, :], dest_f[:, k.slot, :]).then_inc(dest_ready, 1)

            def split_here(k):
                return k.within(1, CH)

            def step(k):
                f, ff, p1, p2 = k.plus(1), k.plus(2), k.plus(-1), k.plus(-2)
                front, back = f.within(0, CH), k.within(0, CH)
                if split_here(ff):
                    split_hi(ff)
                if split_here(ff):
                    split_lo(ff)
                if back:
                    scan(k)
                if p1.within(0, CH):
                    neg_mean_rstd(p1)
                if p2.within(0, CH):
                    places(p2)
                    destinations(p2)
                if front:
                    abs_z(f, 1)
                if p2.within(0, CH):
                    integer_destinations(p2)
                if front:
                    wait(dve, bcd_ready, f.n - 1)
                    dve.tensor_copy(bcd_tok[:, f.slot, 0:2, :].rearrange("p c (b n) -> p c b n", n=N),
                                    zs[:, f.slot, :, D:G0].rearrange("p b (c n) -> p c b n", n=N)).then_inc(delta_ready, 1)
                if p1.within(0, CH):
                    route_top(p1)
                if back:
                    residual_stats(k)
                elif p1.within(0, CH):
                    for part in route(p1):
                        part()
                if front:
                    dve.wait_ge(soft_ready, (f.n + 1) * 2)
                    dve.tensor_tensor(bcd_tok[:, f.slot, 2, :].rearrange("p (b n) -> p b n", n=N),
                                      relu_sum[:, f.slot, :].rearrange("p (b a) -> p b a", a=1).broadcast_to([P, NB, N]),
                                      ln_sum[:, f.slot, :].rearrange("p (b a) -> p b a", a=1).broadcast_to([P, NB, N]),
                                      ALU.add).then_inc(delta_ready, 1)
                if p1.within(0, CH):
                    route_earlier(p1)
                    router_weight_1(p1)
                if back:
                    if ff.within(0, CH) or p1.within(0, CH):
                        dve.wait_ge(stats_ready, (k.n + 1) * NB)
                if ff.within(0, CH):
                    abs_z(ff, 0)
                if p1.within(0, CH):
                    router_weight(p1)
                if back:
                    if not ff.within(0, CH) and not p1.within(0, CH):
                        dve.wait_ge(stats_ready, (k.n + 1) * NB)
                    mean_var(k)

            run_steps(dve, step, -2, *LOOP1, CH + 2, R1)

            dve.wait_ge(ends_ready, 1)
            dve.tensor_copy(ends_i[:, :], ps[:, 0, 0:E]).then_inc(ends_i_ready, 1)
            link(dve.tensor_scalar(tiles_i[:, :], ps[:, 0, 0:E], float(P - 1), None, ALU.add))
            link(dve.tensor_scalar(tiles_i[:, :], tiles_i[:, :], P.bit_length() - 1, None, ALU.logical_shift_right))
            link(dve.tensor_copy(tiles_f[:, :], tiles_i[:, :]))
            link(dve.tensor_tensor(tiles_f[:, :], tiles_f[:, :], region[:, :], ALU.subtract))
            link(dve.tensor_tensor_scan(tiles_in[:, :], ones[:, 0:E], tiles_f[:, :], 0.0, ALU.mult, ALU.add))
            link(dve.tensor_scalar(gap[:, :], tiles_f[:, :], -1.0, float(REGION), ALU.mult, ALU.add))
            per_tile = "p (a e) -> p a e"
            link(dve.tensor_tensor(past[:, :, :], tile_no[:, :].rearrange("p (t a) -> p t a", a=1).broadcast_to([1, ST, E]),
                                   tiles_in[0:1, :].rearrange(per_tile, a=1).broadcast_to([1, ST, E]), ALU.is_ge))
            link(dve.tensor_tensor(past_gap[:, :, :], past[:, :, :], gap[0:1, :].rearrange(per_tile, a=1).broadcast_to([1, ST, E]), ALU.mult))
            link(dve.reduce_sum(source_f[:, :], past_gap[:, :, :], X_AXIS))
            link(dve.tensor_tensor(source_f[:, :], source_f[:, :], tile_no[:, :], ALU.add))
            dve.tensor_scalar(source[:, :], source_f[:, :], float(E * REGION), None, ALU.min).then_inc(source_ready, 1)
            link(dve.reduce_sum(expert_f[:, :], past[:, :, :], X_AXIS))
            dve.tensor_scalar(expert[:, :], expert_f[:, :], float(E - 1), None, ALU.min).then_inc(expert_ready, 1)

            def ffn_step(t):
                cur, res, old = t, t.plus(-RES_LAG), t.plus(-LN_LAG)
                if old.within(0, ST):
                    r = old.c % R3
                    dve.wait_ge(frs_ready, old.n + 1)
                    wait(dve, fout_ready, old.n + 1 - R3)
                    dve.scalar_tensor_tensor(fnm[:, r:r + 1], fmv[:, r, 0:1], -1.0, frs[:, r:r + 1], ALU.mult, ALU.mult)\
                       .then_inc(fnm_ready, 1)
                if res.within(0, ST):
                    r = res.c % R3
                    dve.wait_ge(y_ready, res.n + 1)
                    wait(dve, fout_ready, res.n + 1 - R3)
                    dve.tensor_tensor(x2p[:, r, :], ps[:, 6 + res.c % 2, 0:D], fr[:, res.slot, 0:D], ALU.add).then_inc(x2p_ready, 1)
                    wait(dve, out_stored[res.slot], 16 * res.round)
                    dve.tensor_copy(token[:, res.slot:res.slot + 1], fr[:, res.slot, token_col:token_col + 1].bitcast(i32)).then_inc(tok_ready, 1)
                    dve.wait_ge(x2p_ready, res.n + 1)
                    dve.bn_stats(fst[:, r, :], x2p[:, r, :]).then_inc(fst_ready, 1)
                    dve.wait_ge(fst_ready, res.n + 1)
                if cur.within(0, ST):
                    dve.wait_ge(silu_ready, cur.n + 1)
                    wait(dve, hidt_ready, cur.n - 1)
                    dve.scalar_tensor_tensor(hid[:, cur.c % 2, :], ps[:, cur.c % 2, F:2 * F], fr[:, cur.slot, D:D + 1],
                                             silu_g[:, cur.c % 2, :], ALU.mult, ALU.mult).then_inc(hid_ready, 1)
                if res.within(0, ST):
                    r = res.c % R3
                    dve.bn_aggr(fmv[:, r, :], fst[:, r, :]).then_inc(fmv_ready, 1)
                    dve.wait_ge(fmv_ready, res.n + 1)
                    dve.tensor_scalar(fve[:, r:r + 1], fmv[:, r, 1:2], EPS, None, ALU.add).then_inc(fve_ready, 1)

            run_steps(dve, ffn_step, 0, *LOOP2, ST + LN_LAG, R2)

        @block.tensor
        def _(pe):
            pe.wait_ge(gate_loaded, 48)
            pe.wait_ge(consts_ready, 13)
            for ic in range(KC):
                for jc in range(KC):
                    mm = pe.matmul(ps[:, ic, 0:E], wot_f[:, jc, ic * P:(ic + 1) * P], gwt_f[:, jc, :], start=(jc == 0), stop=(jc == KC - 1))
            mm.then_inc(setup_mm, 1)
            for jc in range(KC):
                pe.matmul(ps[:, 2, 0:E], ones[:, :], gwt_f[:, jc, :], start=(jc == 0), stop=(jc == KC - 1))
            pe.wait_ge(setup_dve, 5)
            for jc in range(KC):
                mm = pe.matmul(ps[:, 3, 0:E], ones[:, :], bogw[:, jc, :], start=(jc == 0), stop=(jc == KC - 1))
            mm.then_inc(setup_mm, 1)
            pe.wait_ge(a_loaded, 32)
            for jc in range(KC):
                mm = pe.matmul(ps[0:Q, 7, 0:1], a4[:, jc, :, :].rearrange("p b n -> p (b n)"), ones[:, 0:1], start=(jc == 0), stop=(jc == KC - 1))
            mm.then_inc(setup_mm, 1)
            pe.wait_ge(setup_dve, 12)

            def products(dst, k, b, w_hi, w_lo, bias):
                tok = slice(b * P, (b + 1) * P)
                terms = [(xh, w_hi), (xh, w_lo), (xl, w_hi)]
                if bias:
                    pe.matmul(dst, two_ones[:, :], bias_hl[:, :], start=True, stop=False)
                for i, (xs, w) in enumerate(terms):
                    for kc in range(KC):
                        mm = pe.matmul(dst, xs[:, k.slot, kc, tok], w[:, kc, :], start=(not bias and i == 0 and kc == 0),
                                       stop=(i == len(terms) - 1 and kc == KC - 1))
                return mm

            def tile_pair(k, p):
                if p == 0:
                    pe.wait_ge(xh_ready, k.n + 1)
                    pe.wait_ge(xl_ready, k.n + 1)
                for b in (2 * p, 2 * p + 1):
                    wait(pe, z_copied, k.n * 2 + p)
                    products(ps[:, b % 2, 0:ZS], k, b, wz_hi, wz_lo, True).then_inc(z_ready, 1)
                if isinstance(k.n, int) and k.n == 0 and p == 0:
                    pe.wait_ge(setup_dve, 13)
                wait(pe, x1p_ready, (k.n - 2) * NB + 2 * p + 2)
                for b in (2 * p, 2 * p + 1):
                    products(ps[:, 2 + 2 * k.slot + p, b % 2 * D:(b % 2 + 1) * D], k, b, wo_hi, wo_lo, False).then_inc(wo_ready, 1)

            def ranks(k):
                pe.wait_ge(onehot_ready, k.n + 1)
                wait(pe, earlier_ready, k.n)
                wait(pe, place_ready, k.n)
                at = ps[:, 7, RANKS:RANKS + NB * E].rearrange("p (b e) -> p b e", e=E)
                pe.matmul(at, below[:, :], picked[:, k.slot, 1:1 + NB, :], start=True, stop=False)
                for b in range(NB):
                    mm = pe.matmul(at[:, b:NB, :], ones[:, :], picked[:, k.slot, b:b + 1, :].broadcast_to([P, NB - b, E]),
                                   start=False, stop=(b == NB - 1))
                mm.then_inc(ranks_ready, 1)

            def step(k):
                f, ff, p1 = k.plus(1), k.plus(2), k.plus(-1)
                front, back = f.within(0, CH), k.within(0, CH)
                if back:
                    pe.wait_ge(delta_ready, (k.n + 1) * 2)
                    wait(pe, bcd_copied, k.n)
                    pe.transpose(ps[:, 6, 0:P], bcd_tok[:, k.slot, 0:2, :].rearrange("p c q -> p (c q)"), ident[:, :])
                    for i in (1, 2):
                        tr = pe.transpose(ps[0:Q, 6, i * P:(i + 1) * P], bcd_tok[:, k.slot, i, :], ident[:, :])
                    tr.then_inc(bcd_ready, 1)
                if front:
                    tile_pair(f, 1)
                if back:
                    pe.wait_ge(hc_ready, k.n + 1)
                    wait(pe, s_copied, k.n)
                    wait(pe, place_ready, k.n - 1)
                    pe.matmul(ps[:, 7, 0:NB], hc[:, k.slot, :], batch_sel[:, :], start=True, stop=True).then_inc(s_ready, 1)
                if ff.within(0, CH):
                    tile_pair(ff, 0)
                if p1.within(0, CH):
                    wait(pe, s_copied, k.n + 1 if back else CH)
                    ranks(p1)

            run_steps(pe, step, -2, *LOOP1, CH + 1, R1)

            pe.wait_ge(earlier_ready, CH)
            pe.matmul(ps[:, 0, 0:E], ones[:, :], picked[:, CH % R1, 0, :], start=True, stop=True).then_inc(ends_ready, 1)

            pe.wait_ge(expert_ready, 1)
            pe.wait_ge(moe_loaded, 32 * CH)

            def load_expert(j):
                return nc.s_assert_within(pe.value_load(expert[0:1, bass.ds(j.n, 1)]), 0, E - 1,
                                          skip_runtime_bounds_check_because="a count of experts, cut off at E - 1")

            def ffn_step(t):
                cur, nxt, prev, old = t, t.plus(1), t.plus(-2), t.plus(-3)
                if old.within(0, ST):
                    e_old = load_expert(old)
                if cur.within(0, ST):
                    e_cur = load_expert(cur)
                if nxt.within(0, ST):
                    h = nxt.c % 2
                    pe.wait_ge(fr_loaded[nxt.slot], 16 * (nxt.round + 1))
                    wait(pe, fxt_copied, nxt.n - 1)
                    for kc in range(KC):
                        tr = pe.transpose(ps[:, 2 + h, kc * P:(kc + 1) * P], fr[:, nxt.slot, kc * P:(kc + 1) * P], ident[:, :])
                    tr.then_inc(fxt_ready, 1)
                if prev.within(0, ST):
                    h = prev.c % 2
                    pe.wait_ge(hid_ready, prev.n + 1)
                    wait(pe, hidt_copied, prev.n - 1)
                    pe.transpose(ps[:, 4 + h, 0:P], hid[:, h, :], ident[:, :]).then_inc(hidt_ready, 1)
                if old.within(0, ST):
                    h = old.c % 2
                    pe.wait_ge(hidt_copied, old.n + 1)
                    wait(pe, x2p_ready, old.n - 1)
                    pe.matmul(ps[:, 6 + h, 0:D], hidt[:, h, :], w_dn[:, bass.ds(e_old, 1), :].rearrange("p a n -> p (a n)"),
                              start=True, stop=True).then_inc(y_ready, 1)
                if cur.within(0, ST):
                    h = cur.c % 2
                    pe.wait_ge(fxt_copied, cur.n + 1)
                    wait(pe, hid_ready, cur.n - 1)
                    for kc in range(KC):
                        mm = pe.matmul(ps[:, h, 0:2 * F], fxt[:, cur.c % R3, kc, :], w_gu[:, bass.ds(e_cur, 1), kc, :].rearrange("p a n -> p (a n)"),
                                       start=(kc == 0), stop=(kc == KC - 1))
                    mm.then_inc(gu_ready, 1)

            run_steps(pe, ffn_step, -1, *LOOP2, ST + 3, R2)


def kernel(**inputs):
    import numpy as _np
    import concourse.bacc as _bacc
    from concourse import mybir as _mybir
    from concourse.bass_utils import run_bass_kernel_spmd as _run

    i = {k.removeprefix("L0_"): _np.asarray(v) for k, v in inputs.items()}
    x = i["attn_x"]
    nb, t, d = x.shape
    p = 128
    n_exp, f, _ = i["ffn_w_gate"].shape
    xt = x.reshape(nb, t // p, p, d // p, p).transpose(1, 4, 3, 0, 2).reshape(t // p, p, d // p, nb * p)
    wgu = _np.stack([i["ffn_w_gate"], i["ffn_w_up"]], axis=1)
    wgu = wgu.reshape(n_exp, 2, f, d // p, p).transpose(4, 0, 3, 1, 2).reshape(p, n_exp, d // p, 2 * f)
    given = {
        "x": x, "xt": xt, "wd": i["attn_Wd"], "wb": i["attn_Wb"], "wc": i["attn_Wc"], "wo": i["attn_Wo"], "wot": i["attn_Wo"].T,
        "bd": i["attn_bd"], "bb": i["attn_bb"], "bc": i["attn_bc"], "bo": i["attn_bo"], "bo_cols": i["attn_bo"].reshape(d // p, p).T, "a_mat": i["attn_A"],
        "gwt": i["ffn_gate_w"].T, "wgu": wgu, "wdn": i["ffn_w_down"].transpose(0, 2, 1),
    }
    nc = _bacc.Bacc("TRN2", target_bir_lowering=False, num_devices=1)
    arrays, args = {}, {}
    for name, a in given.items():
        a = _np.ascontiguousarray(a)
        arrays[f"in_{name}"] = a
        args[name] = nc.dram_tensor(f"in_{name}", a.shape, _mybir.dt.from_np(a.dtype), kind="ExternalInput").ap()
    args["out"] = nc.dram_tensor("out", (nb * t, d), _mybir.dt.float32, kind="ExternalOutput").ap()
    ssm_attention_then_top1_moe(nc, **args)
    r = _run(nc, [arrays], core_ids=[0])
    return r.results[0]["out"].reshape(nb, t, d)
```

```python
import concourse.bass as bass
from concourse import mybir
from contextlib import ExitStack


class Step:

    def __init__(self, turn, c, ring):
        self.turn, self.c, self.ring = turn, c, ring
        self.n = turn * ring + c
        self.slot = c % ring
        self.round = turn + c // ring

    def plus(self, d):
        return Step(self.turn, self.c + d, self.ring)

    def within(self, lo, hi):
        return not isinstance(self.n, int) or lo <= self.n < hi


def run_steps(engine, body, first, loop_from, loop_to, last, ring):
    for n in range(first, loop_from):
        body(Step(0, n, ring))
    if loop_to > loop_from:
        with engine.Fori(0, (loop_to - loop_from) // ring) as turn:
            for u in range(ring):
                body(Step(turn, loop_from + u, ring))
    for n in range(loop_to, last):
        body(Step(0, n, ring))


def wait(engine, sem, value):
    if not isinstance(value, int) or value > 0:
        engine.wait_ge(sem, value)


def ssm_attention_then_top1_moe(nc: bass.Bass, x, xt, wdbc, wo, gate_pack, bias_rows, bo, a_tiled, wgu, wdn, out):
    fp32, fp32r, i32 = mybir.dt.float32, mybir.dt.float32r, mybir.dt.int32
    ALU = mybir.AluOpType
    ACT = mybir.ActivationFunctionType
    X_AXIS = mybir.AxisListType.X

    P = 128
    NB, T, D = x.shape
    N = (wdbc.shape[1] - D) // 2
    E = wgu.shape[1]
    F = wdn.shape[1]
    KC = D // P
    CH = T // P
    TILES = CH * NB
    TOK = NB * T
    Q = NB * N
    ZS = D + 2 * N + 2 * E
    G0 = D + 2 * N
    ROW = D + 2
    ST = TILES + E - 1
    EPS = 1e-5
    NO_TOKEN = 1 << 20
    REGION = TILES + 1
    R1, R2 = 2, 8
    R3 = 4
    RES_LAG, STD_LAG, LN_LAG, OUT_LAG = 4, 5, 6, 7

    ctx = ExitStack()
    with ctx:
        def sb(name, shape, dt=fp32):
            return ctx.enter_context(nc.sbuf_tensor(name, shape, dt))

        def sem(name):
            return ctx.enter_context(nc.semaphore(name))

        wz = sb("wz", [P, KC, ZS])
        wz_hi, wz_lo = sb("wz_hi", [P, KC, ZS], fp32r), sb("wz_lo", [P, KC, ZS], fp32r)
        wo_f = sb("wo_f", [P, KC, D])
        wo_hi, wo_lo = sb("wo_hi", [P, KC, D], fp32r), sb("wo_lo", [P, KC, D], fp32r)
        gates = sb("gates", [P, KC, D + E + 1])
        wot_f, gwt_f, bo_col = gates[:, :, 0:D], gates[:, :, D:D + E], gates[:, :, D + E]
        bogw = sb("bogw", [P, KC, E])
        bo_row = sb("bo_row", [P, D])
        bias_f, bias_hl = sb("bias_f", [2, ZS]), sb("bias_hl", [P, ZS], fp32r)
        two_ones = sb("two_ones", [P, P], fp32r)
        a4 = sb("a4", [P, KC, NB, N])
        ident, ones, below = sb("ident", [P, P]), sb("ones", [P, P]), sb("below", [P, P])
        ones_r, below_r = sb("ones_r", [P, P], fp32r), sb("below_r", [P, P], fp32r)
        batch_sel = sb("batch_sel", [Q, NB])
        sig_a = sb("sig_a", [Q, 2])
        gate_sum = sb("gate_sum", [P, E])
        falling, region = sb("falling", [P, E]), sb("region", [P, E])
        falling_i, region_i = sb("falling_i", [P, E], i32), sb("region_i", [P, E], i32)
        tile_no, tile_no_i = sb("tile_no", [1, ST]), sb("tile_no_i", [1, ST], i32)
        minus_half = sb("minus_half", [P, NB])
        empty_row = sb("empty_row", [P, ROW])
        w_gu, w_dn = sb("w_gu", [P, E, KC, 2 * F]), sb("w_dn", [P, E, D])

        xr, xts = sb("xr", [P, R1, NB, D]), sb("xts", [P, R1, KC, NB * P])
        xh, xl = sb("xh", [P, R1, KC, NB * P], fp32r), sb("xl", [P, R1, KC, NB * P], fp32r)
        xbo = sb("xbo", [P, R1, NB, D])
        zs = sb("zs", [P, R1, NB, ZS])
        az = sb("az", [P, R1, NB, D])
        relu_z = sb("relu_z", [P, R1, NB, D])
        relu_sum, ln_sum = sb("relu_sum", [P, R1, NB]), sb("ln_sum", [P, R1, NB])
        bcd_tok = sb("bcd_tok", [P, R1, 3, NB * N])
        bcd = sb("bcd", [Q, R1, 3, P])
        keep_h, drive, hs, hc = (sb(n, [Q, R1, P]) for n in ("keep_h", "drive", "hs", "hc"))
        s_tok = sb("s_tok", [P, R1, NB])
        x1p = sb("x1p", [P, R1, NB, D])
        stats, mv = sb("stats", [P, R1, NB, 6]), sb("mv", [P, R1, NB, 2])
        var_eps = sb("var_eps", [P, R1, NB])
        lg1, lg2, lg3 = (sb(n, [P, R1, NB, E]) for n in ("lg1", "lg2", "lg3"))
        rstd, nmr = sb("rstd", [P, R1, NB]), sb("nmr", [P, R1, NB])
        logits = sb("logits", [P, R1, NB, E])
        rows = sb("rows", [P, R1, NB, ROW])

        top, pick, candidates = sb("top", [P, R1, NB]), sb("pick", [P, R1, NB]), sb("candidates", [P, R1, NB, E])
        picked = sb("picked", [P, R1, 1 + NB, E], fp32r)
        place, dest_f, dest = sb("place", [P, R1, NB, E]), sb("dest_f", [P, R1, NB]), sb("dest", [P, R1, NB], i32)
        rw_t, rw_e, rw_1 = (sb(n, [P, R1, NB]) for n in ("rw_t", "rw_e", "rw_1"))
        ends_i, tiles_i, tiles_f, tiles_in, gap = (sb("ends_i", [P, E], i32), sb("tiles_i", [P, E], i32), sb("tiles_f", [P, E]),
                                                   sb("tiles_in", [P, E]), sb("gap", [P, E]))
        past, past_gap = sb("past", [1, ST, E]), sb("past_gap", [1, ST, E])
        expert_f, expert = sb("expert_f", [1, ST]), sb("expert", [1, ST], i32)
        source_f, source = sb("source_f", [1, ST]), sb("source", [1, ST], i32)

        fr = sb("fr", [P, R2, ROW])
        fxt = sb("fxt", [P, R3, KC, P])
        silu_g, hid = sb("silu_g", [P, 2, F]), sb("hid", [P, 2, F])
        hidt = sb("hidt", [P, 2, P])
        x2p = sb("x2p", [P, R3, D])
        fst, fmv, fve, frs, fnm = sb("fst", [P, R3, 6]), sb("fmv", [P, R3, 2]), sb("fve", [P, R3]), sb("frs", [P, R3]), sb("fnm", [P, R3])
        token = sb("token", [P, R2], i32)
        fout = sb("fout", [P, R2, D])

        ps = ctx.enter_context(nc.psum_tensor("ps", [P, 8, 512], fp32))
        sorted_rows = nc.dram_tensor("sorted_rows", ((E * REGION + 1) * P, ROW), fp32).ap()
        token_col = D + 1
        RANKS = 64

        wz_loaded, wo_loaded, gate_loaded, bias_loaded = sem("wz_loaded"), sem("wo_loaded"), sem("gate_loaded"), sem("bias_loaded")
        a_loaded, bo_loaded, moe_loaded = sem("a_loaded"), sem("bo_loaded"), sem("moe_loaded")
        x_loaded, xt_loaded = [sem(f"x_loaded{i}") for i in range(R1)], [sem(f"xt_loaded{i}") for i in range(R1)]
        consts_ready, empty_ready, empty_stored = sem("consts_ready"), sem("empty_ready"), sem("empty_stored")
        setup_mm, setup_dve, setup_act = sem("setup_mm"), sem("setup_dve"), sem("setup_act")
        xh_ready, xl_ready, xbo_ready = sem("xh_ready"), sem("xl_ready"), sem("xbo_ready")
        z_ready, wo_ready, z_copied = sem("z_ready"), sem("wo_ready"), sem("z_copied")
        abs_ready, exp_ready, soft_ready = sem("abs_ready"), sem("exp_ready"), sem("soft_ready")
        delta_ready, bcd_ready, bcd_copied = sem("delta_ready"), sem("bcd_ready"), sem("bcd_copied")
        keep_ready, drive_ready, h_ready, hc_ready = sem("keep_ready"), sem("drive_ready"), sem("h_ready"), sem("hc_ready")
        s_ready, s_copied, x1p_ready, stats_ready, mv_ready = sem("s_ready"), sem("s_copied"), sem("x1p_ready"), sem("stats_ready"), sem("mv_ready")
        var_ready, rstd_ready, nmr_ready, norm_ready = sem("var_ready"), sem("rstd_ready"), sem("nmr_ready"), sem("norm_ready")
        lg1_ready, lg2_ready, lg3_ready, logits_ready = sem("lg1_ready"), sem("lg2_ready"), sem("lg3_ready"), sem("logits_ready")
        route_step, top_ready, cand_ready, first_ready, pick_ready = sem("route_step"), sem("top_ready"), sem("cand_ready"), sem("first_ready"), sem("pick_ready")
        onehot_ready, earlier_ready, ranks_ready, place_ready, dest_f_ready, dest_ready = sem("onehot_ready"), sem("earlier_ready"), sem("ranks_ready"), sem("place_ready"), sem("dest_f_ready"), sem("dest_ready")
        rw_t_ready, rw_exp_ready, rw_1_ready, rw_ready, token_ready = sem("rw_t_ready"), sem("rw_exp_ready"), sem("rw_1_ready"), sem("rw_ready"), sem("token_ready")
        rows_scattered = [sem(f"rows_scattered{i}") for i in range(R1)]
        ends_ready, ends_i_ready, expert_ready, source_ready, pads_stored = sem("ends_ready"), sem("ends_i_ready"), sem("expert_ready"), sem("source_ready"), sem("pads_stored")
        fr_loaded = [sem(f"fr_loaded{i}") for i in range(R2)]
        fxt_ready, fxt_copied, gu_ready, silu_ready, hid_ready = sem("fxt_ready"), sem("fxt_copied"), sem("gu_ready"), sem("silu_ready"), sem("hid_ready")
        hidt_ready, hidt_copied, y_ready, x2p_ready, fst_ready, fmv_ready = sem("hidt_ready"), sem("hidt_copied"), sem("y_ready"), sem("x2p_ready"), sem("fst_ready"), sem("fmv_ready")
        tok_ready = sem("tok_ready")
        fve_ready, frs_ready, fnm_ready, fout_ready = sem("fve_ready"), sem("frs_ready"), sem("fnm_ready"), sem("fout_ready")
        out_stored = [sem(f"out_stored{i}") for i in range(R2)]

        LOOP1 = (4, 6)
        LOOP2 = (R2 + OUT_LAG, R2 + OUT_LAG + (ST - 1 - R2 - OUT_LAG) // R2 * R2)
        x_v = x.rearrange("b (c p) d -> c p b d", p=P)

        def pad_regions(engine, experts):
            engine.wait_ge(ends_i_ready, 1)
            for e in experts:
                end = nc.s_assert_within(engine.value_load(ends_i[0:1, e:e + 1]), 0, E * REGION * P,
                                         skip_runtime_bounds_check_because="a region's first row plus at most every token")
                engine.dma_start(sorted_rows[bass.ds(end, P), :], empty_row[:, :]).then_inc(pads_stored, 16)

        def on_idle_vector(k):
            return isinstance(k.n, int) and k.n == CH - 1

        block = ctx.enter_context(nc.Block())

        @block.sync
        def _(sp):
            def load_xt(k):
                wait(sp, xh_ready, k.n - 1)
                wait(sp, xl_ready, k.n - 1)
                sp.dma_start(xts[:, k.slot, :, :], xt[bass.ds(k.n, 1), :, :, :].rearrange("c p k t -> p (c k) t"))\
                  .then_inc(xt_loaded[k.slot], 16)

            def load_x(k):
                wait(sp, xbo_ready, (k.n - 1) * 2)
                sp.dma_start(xr[:, k.slot, :, :], x_v[bass.ds(k.n, 1), :, :, :].rearrange("c p b d -> p (c b) d"))\
                  .then_inc(x_loaded[k.slot], 16)

            def load_moe(k):
                some = bass.ds(k.n * (E // CH), E // CH)
                sp.dma_start(w_gu[:, some, :, :], wgu[:, some, :, :]).then_inc(moe_loaded, 16)
                sp.dma_start(w_dn[:, some, :], wdn[some, :, :].rearrange("e f d -> f e d")).then_inc(moe_loaded, 16)

            def load_chunk(k):
                if k.within(0, CH):
                    load_xt(k)
                    load_x(k)
                load_moe(k.plus(-1))

            load_xt(Step(0, 0, R1))
            sp.dma_start(wz[:, :, 0:G0], wdbc.rearrange("(k p) n -> p k n", p=P)).then_inc(wz_loaded, 16)
            sp.dma_start(wo_f[:, :, :], wo.rearrange("(k p) n -> p k n", p=P)).then_inc(wo_loaded, 16)
            load_x(Step(0, 0, R1))
            run_steps(sp, load_chunk, 1, *LOOP1, CH + 1, R1)

            pad_regions(sp, range(0, E // 2))

            sp.wait_ge(source_ready, 1)
            sp.wait_ge(pads_stored, 16 * E)
            sp.wait_ge(empty_stored, 16)
            for s in range(R1):
                sp.wait_ge(rows_scattered[s], 16 * NB * CH // R1)

            def load_tile(j):
                if not j.within(0, ST):
                    return
                at = nc.s_assert_within(sp.value_load(source[0:1, bass.ds(j.n, 1)]), 0, E * REGION,
                                        skip_runtime_bounds_check_because="a sum of counts, cut off at the tile of empty rows")
                wait(sp, x2p_ready, j.n + 1 - R2)
                wait(sp, tok_ready, j.n + 1 - R2)
                sp.dma_start(fr[:, j.slot, :], sorted_rows.rearrange("(t p) r -> t p r", p=P)[bass.ds(at, 1), :, :].rearrange("t p r -> p (t r)"))\
                  .then_inc(fr_loaded[j.slot], 16)

            run_steps(sp, load_tile, 0, *LOOP2, ST, R2)
            for s in range(R2):
                sp.wait_ge(out_stored[s], 16 * len(range(s, ST, R2)))

        @block.scalar
        def _(act):
            act.preload_act_table_set("natural_log_exp_and_others")
            act.dma_start(gates[:, :, :], gate_pack.rearrange("(k p) n -> p k n", p=P)).then_inc(gate_loaded, 16)
            act.dma_start(bias_f[0:2, 0:G0], bias_rows).then_inc(bias_loaded, 16)
            act.dma_start(a4[:, :, :, :], a_tiled.rearrange("(k p) b n -> p k b n", p=P)).then_inc(a_loaded, 16)
            act.dma_start(bo_row[:, :], bo.rearrange("(a n) -> a n", a=1).broadcast_to([P, D])).then_inc(bo_loaded, 16)
            act.wait_ge(empty_ready, 2)
            act.dma_start(sorted_rows[E * REGION * P:(E * REGION + 1) * P, :], empty_row[:, :]).then_inc(empty_stored, 16)

            def copy_z(k, p):
                act.wait_ge(z_ready, k.n * NB + 2 * p + 2)
                wait(act, delta_ready, (k.n - 1) * 2)
                wait(act, lg2_ready, k.n - 1)
                act.activation(zs[:, k.slot, 2 * p:2 * p + 2, :], ps[:, 0:2, 0:ZS], ACT.Copy).then_inc(z_copied, 1)

            def softplus(k, p):
                pair = az[:, k.slot, 2 * p:2 * p + 2, :]
                act.wait_ge(abs_ready, k.n * 2 + p + 1)
                act.activation(pair, pair, ACT.Exp, scale=-1.0).then_inc(exp_ready, 1)
                for b in (2 * p, 2 * p + 1):
                    act.activation(relu_z[:, k.slot, b, :], zs[:, k.slot, b, 0:D], ACT.Relu, accum_out=relu_sum[:, k.slot, b:b + 1])
                act.wait_ge(exp_ready, k.n * 2 + p + 1)
                for b in (2 * p, 2 * p + 1):
                    last = act.activation(az[:, k.slot, b, :], az[:, k.slot, b, :], ACT.Ln, bias=1.0,
                                          accum_out=ln_sum[:, k.slot, b:b + 1])
                last.then_inc(soft_ready, 1)

            def normalize(k):
                act.wait_ge(nmr_ready, k.n + 1)
                wait(act, rows_scattered[k.slot], 16 * NB * k.round)
                for b in range(NB):
                    act.activation(rows[:, k.slot, b, 0:D], x1p[:, k.slot, b, :], ACT.Identity,
                                   bias=nmr[:, k.slot, b:b + 1], scale=rstd[:, k.slot, b:b + 1]).then_inc(norm_ready, 1)

            def router_exp(k):
                act.wait_ge(rw_t_ready, k.n + 1)
                wait(act, rw_1_ready, k.n - 1)
                act.activation(rw_e[:, k.slot, :], rw_t[:, k.slot, :], ACT.Exp, scale=-1.0).then_inc(rw_exp_ready, 1)

            def step(k):
                f, ff, p1 = k.plus(1), k.plus(2), k.plus(-1)
                if k.within(0, CH):
                    act.wait_ge(bcd_ready, k.n + 1)
                    act.activation(bcd[:, k.slot, :, :], ps[0:Q, 6, 0:3 * P].rearrange("q (a t) -> q a t", a=3), ACT.Copy)\
                       .then_inc(bcd_copied, 1)
                if f.within(0, CH):
                    softplus(f, 0)
                    copy_z(f, 1)
                    softplus(f, 1)
                if ff.within(0, CH):
                    copy_z(ff, 0)
                if p1.within(0, CH):
                    router_exp(p1)
                    normalize(p1)

            step(Step(0, -2, R1))
            act.wait_ge(setup_mm, 3)
            act.activation(sig_a[:, 0:1], ps[0:Q, 7, 0:1], ACT.Exp, scale=-1.0 / D).then_inc(setup_act, 1)
            run_steps(act, step, -1, *LOOP1, CH + 1, R1)

            pad_regions(act, range(E // 2, E))
            act.preload_act_table_set("silu_and_others")

            def ffn_step(t):
                nxt, cur, prev, old = t.plus(1), t, t.plus(-2), t.plus(-LN_LAG)
                if nxt.within(0, ST):
                    act.wait_ge(fxt_ready, nxt.n + 1)
                    wait(act, gu_ready, nxt.n + 1 - R3)
                    act.activation(fxt[:, nxt.c % R3, :, :], ps[:, 2 + nxt.c % 2, 0:D].rearrange("p (k t) -> p k t", k=KC), ACT.Copy)\
                       .then_inc(fxt_copied, 1)
                if prev.within(0, ST):
                    act.wait_ge(hidt_ready, prev.n + 1)
                    wait(act, y_ready, prev.n - 1)
                    act.activation(hidt[:, prev.c % 2, :], ps[:, 4 + prev.c % 2, 0:P], ACT.Copy).then_inc(hidt_copied, 1)
                if cur.within(0, ST):
                    act.wait_ge(gu_ready, cur.n + 1)
                    wait(act, hid_ready, cur.n - 1)
                    act.activation(silu_g[:, cur.c % 2, :], ps[:, cur.c % 2, 0:F], ACT.Silu, scale=fr[:, cur.slot, D:D + 1])\
                       .then_inc(silu_ready, 1)
                if old.within(0, ST):
                    r = old.c % R3
                    act.wait_ge(fnm_ready, old.n + 1)
                    wait(act, out_stored[old.slot], 16 * old.round)
                    act.activation(fout[:, old.slot, :], x2p[:, r, :], ACT.Identity, bias=fnm[:, r:r + 1],
                                   scale=frs[:, r:r + 1]).then_inc(fout_ready, 1)

            run_steps(act, ffn_step, -1, *LOOP2, ST + LN_LAG, R2)

        @block.gpsimd
        def _(pool):
            pool.memset(empty_row[:, :], 0.0).then_inc(empty_ready, 1)
            pool.wait_ge(empty_ready, 1)
            pool.memset(empty_row[:, token_col:token_col + 1].bitcast(i32), NO_TOKEN).then_inc(empty_ready, 1)
            pool.memset(ident[:, :], 0.0).then_inc(consts_ready, 1)
            pool.memset(ones[:, :], 1.0).then_inc(consts_ready, 1)
            pool.memset(below[:, :], 1.0).then_inc(consts_ready, 1)
            pool.memset(batch_sel[:, :], 1.0).then_inc(consts_ready, 1)
            pool.iota(falling_i[:, :], pattern=[[-1, E]], base=E, channel_multiplier=0).then_inc(consts_ready, 1)
            pool.iota(region_i[:, :], pattern=[[REGION, E]], base=0, channel_multiplier=0).then_inc(consts_ready, 1)
            pool.iota(tile_no_i[:, :], pattern=[[1, ST]], base=0, channel_multiplier=0).then_inc(consts_ready, 1)
            pool.iota(rows[:, :, :, token_col:token_col + 1].bitcast(i32),
                      pattern=[[P, R1], [T, NB], [1, 1]], base=-R1 * P, channel_multiplier=1).then_inc(consts_ready, 1)
            pool.memset(minus_half[:, :], -0.5).then_inc(consts_ready, 1)
            pool.wait_ge(consts_ready, 9)
            pool.affine_select(out=ident[:, :], in_=ident[:, :], compare_op=ALU.not_equal, fill=1.0, base=0,
                               pattern=[[-1, P]], channel_multiplier=1).then_inc(consts_ready, 1)
            pool.affine_select(out=below[:, :], in_=below[:, :], compare_op=ALU.is_gt, fill=0.0, base=0,
                               pattern=[[1, P]], channel_multiplier=-1).then_inc(consts_ready, 1)
            pool.affine_select(out=batch_sel[:, :], in_=batch_sel[:, :], compare_op=ALU.is_ge, fill=0.0, base=0,
                               pattern=[[-N, NB]], channel_multiplier=1).then_inc(consts_ready, 1)
            pool.wait_ge(consts_ready, 12)
            pool.affine_select(out=batch_sel[:, :], in_=batch_sel[:, :], compare_op=ALU.is_ge, fill=0.0, base=N - 1,
                               pattern=[[N, NB]], channel_multiplier=-1).then_inc(consts_ready, 1)

            def spread(v):
                return v.rearrange("p (b a) -> p b a", a=1).broadcast_to([P, NB, E])

            def logits_of_products(k):
                if k.within(0, CH):
                    pool.wait_ge(s_copied, k.n + 1)
                    pool.wait_ge(z_copied, (k.n + 1) * 2)
                    wait(pool, lg2_ready, k.n)
                    pool.tensor_tensor(lg1[:, k.slot, :, :], zs[:, k.slot, :, G0 + E:ZS], spread(s_tok[:, k.slot, :]), ALU.mult).then_inc(lg1_ready, 1)
                    pool.wait_ge(lg1_ready, k.n + 1)
                    wait(pool, logits_ready, k.n - 1)
                    pool.tensor_tensor(lg2[:, k.slot, :, :], lg1[:, k.slot, :, :], zs[:, k.slot, :, G0:G0 + E], ALU.add).then_inc(lg2_ready, 1)

            pool.wait_ge(xh_ready, 1)
            pool.tensor_tensor(xl[:, 0, :, :], xts[:, 0, :, :], xh[:, 0, :, :].bitcast(fp32), ALU.subtract).then_inc(xl_ready, 1)

            def step(k):
                f, p1, p2 = k.plus(1), k.plus(-1), k.plus(-2)
                vector_adds_bo = on_idle_vector(f)
                if p1.within(0, CH):
                    pool.wait_ge(mv_ready, (p1.n + 1) * NB)
                    wait(pool, cand_ready, p1.n - 1)
                    pool.tensor_tensor(lg3[:, p1.slot, :, :], gate_sum[:, :].rearrange("p (a e) -> p a e", a=1).broadcast_to([P, NB, E]),
                                       spread(mv[:, p1.slot, :, 0]), ALU.mult).then_inc(lg3_ready, 1)
                    pool.wait_ge(lg3_ready, p1.n + 1)
                    pool.wait_ge(lg2_ready, p1.n + 1)
                    pool.tensor_tensor(logits[:, p1.slot, :, :], lg2[:, p1.slot, :, :], lg3[:, p1.slot, :, :], ALU.subtract)\
                        .then_inc(logits_ready, 1)
                    pool.wait_ge(var_ready, p1.n + 1)
                    wait(pool, norm_ready, (p1.n - 1) * NB)
                    wait(pool, rw_t_ready, p1.n - 1)
                    pool.tensor_tensor(rstd[:, p1.slot, :], var_eps[:, p1.slot, :], minus_half[:, :], ALU.pow).then_inc(rstd_ready, 1)

                def add_bo(lo, hi):
                    pool.tensor_tensor(xbo[:, f.slot, lo:hi, :], xr[:, f.slot, lo:hi, :],
                                       bo_row[:, :].rearrange("p (a d) -> p a d", a=1).broadcast_to([P, hi - lo, D]), ALU.add)\
                        .then_inc(xbo_ready, 1)

                if f.within(0, CH) and not vector_adds_bo:
                    pool.wait_ge(x_loaded[f.slot], 16 * (f.round + 1))
                    if isinstance(f.n, int) and f.n == 0:
                        pool.wait_ge(bo_loaded, 16)
                    wait(pool, x1p_ready, (f.n - 1) * NB)
                    add_bo(0, NB // 2)
                if f.within(0, CH):
                    logits_of_products(k)
                if p2.within(0, CH):
                    pool.wait_ge(norm_ready, (p2.n + 1) * NB)
                    pool.wait_ge(rw_ready, p2.n + 1)
                    wait(pool, token_ready, p2.n + 1)
                    pool.wait_ge(dest_ready, p2.n + 1)
                if f.within(0, CH) and not vector_adds_bo:
                    add_bo(NB // 2, NB)
                if p2.within(0, CH):
                    for b in range(NB):
                        pool.indirect_dma_start(sorted_rows[:, :], bass.IndirectOffsetOnAxis(dest[:, p2.slot, b:b + 1], axis=0),
                                                rows[:, p2.slot, b, :], None).then_inc(rows_scattered[p2.slot], 16)
                if not f.within(0, CH):
                    logits_of_products(k)

            run_steps(pool, step, -1, *LOOP1, CH + 2, R1)

            def ffn_step(t):
                std, old = t.plus(-STD_LAG), t.plus(-OUT_LAG)
                if old.within(0, ST):
                    pool.wait_ge(fout_ready, old.n + 1)
                    pool.wait_ge(tok_ready, old.n + 1)
                if std.within(0, ST):
                    r = std.c % R3
                    pool.wait_ge(fve_ready, std.n + 1)
                    wait(pool, fout_ready, std.n + 1 - R3)
                    pool.tensor_tensor(frs[:, r:r + 1], fve[:, r:r + 1], minus_half[:, 0:1], ALU.pow).then_inc(frs_ready, 1)
                if old.within(0, ST):
                    pool.indirect_dma_start(out[:, :], bass.IndirectOffsetOnAxis(token[:, old.slot:old.slot + 1], axis=0),
                                            fout[:, old.slot, :], None, bounds_check=TOK - 1, oob_is_err=False)\
                        .then_inc(out_stored[old.slot], 16)

            run_steps(pool, ffn_step, STD_LAG, *LOOP2, ST + OUT_LAG, R2)

        @block.vector
        def _(dve):
            linked = [0]

            def link(ins):
                linked[0] += 1
                ins.then_inc(route_step, 1)
                dve.wait_ge(route_step, linked[0])

            dve.memset(bias_hl[:, :].bitcast(fp32), 0.0).then_inc(setup_dve, 1)
            dve.memset(two_ones[:, :].bitcast(fp32), 0.0).then_inc(setup_dve, 1)
            dve.memset(hs[:, 1, :], 0.0).then_inc(setup_dve, 1)
            dve.wait_ge(setup_dve, 3)
            link(dve.memset(two_ones[0:2, :].bitcast(fp32), 1.0))
            dve.wait_ge(consts_ready, 13)
            link(dve.tensor_copy(falling[:, :], falling_i[:, :]))
            link(dve.tensor_copy(tile_no[:, :], tile_no_i[:, :]))
            link(dve.tensor_copy(region[:, :], region_i[:, :]))
            link(dve.tensor_copy(picked[:, 0, 0, :], region[:, :]))
            link(dve.tensor_copy(ones_r[:, :], ones[:, :]))
            link(dve.tensor_copy(below_r[:, :], below[:, :]))
            def split_hi(k):
                dve.wait_ge(xt_loaded[k.slot], 16 * (k.round + 1))
                wait(dve, wo_ready, (k.n - 1) * NB)
                dve.tensor_copy(xh[:, k.slot, :, :], xts[:, k.slot, :, :]).then_inc(xh_ready, 1)

            def split_lo(k):
                dve.wait_ge(xh_ready, k.n + 1)
                dve.tensor_tensor(xl[:, k.slot, :, :], xts[:, k.slot, :, :], xh[:, k.slot, :, :].bitcast(fp32), ALU.subtract)\
                   .then_inc(xl_ready, 1)

            def split_weights(hi, lo, w):
                link(dve.tensor_copy(hi, w))
                dve.tensor_tensor(lo, w, hi.bitcast(fp32), ALU.subtract).then_inc(setup_dve, 1)

            dve.wait_ge(gate_loaded, 16)
            for kc in range(KC):
                dve.tensor_scalar(bogw[:, kc, :], gwt_f[:, kc, :], bo_col[:, kc:kc + 1], None, ALU.mult).then_inc(setup_dve, 1)

            def split_bias(lo, hi):
                link(dve.tensor_copy(bias_hl[0:2, lo:hi], bias_f[:, lo:hi]))
                link(dve.tensor_tensor(bias_hl[0:2, lo:hi], bias_f[:, lo:hi], bias_hl[0:2, lo:hi].bitcast(fp32), ALU.subtract))
                dve.tensor_copy(bias_hl[0:1, lo:hi], bias_f[0:1, lo:hi]).then_inc(setup_dve, 1)

            split_hi(Step(0, 0, R1))
            dve.wait_ge(wz_loaded, 16)
            split_weights(wz_hi[:, :, 0:G0], wz_lo[:, :, 0:G0], wz[:, :, 0:G0])
            dve.wait_ge(bias_loaded, 16)
            split_bias(0, G0)
            dve.wait_ge(setup_mm, 1)
            dve.tensor_copy(wz[:, :, G0:G0 + E], gwt_f).then_inc(setup_dve, 1)
            link(dve.tensor_copy(wz[:, :, G0 + E:ZS], ps[:, 0:KC, 0:E]))
            dve.wait_ge(setup_dve, 8)
            split_weights(wz_hi[:, :, G0:ZS], wz_lo[:, :, G0:ZS], wz[:, :, G0:ZS])
            dve.wait_ge(setup_mm, 2)
            dve.memset(bias_f[0:2, G0 + E:ZS], 0.0).then_inc(setup_dve, 1)
            dve.tensor_copy(gate_sum[:, :], ps[:, 2, 0:E]).then_inc(setup_dve, 1)
            link(dve.tensor_copy(bias_f[0:2, G0:G0 + E], ps[0:2, 3, 0:E]))
            dve.wait_ge(setup_dve, 11)
            split_bias(G0, ZS)
            dve.wait_ge(wo_loaded, 16)
            split_weights(wo_hi[:, :, :], wo_lo[:, :, :], wo_f[:, :, :])

            def abs_z(k, p):
                pair = zs[:, k.slot, 2 * p:2 * p + 2, 0:D]
                dve.wait_ge(z_copied, k.n * 2 + p + 1)
                dve.tensor_scalar(az[:, k.slot, 2 * p:2 * p + 2, :].bitcast(i32), pair.bitcast(i32), 0x7FFFFFFF, None, ALU.bitwise_and)\
                   .then_inc(abs_ready, 1)

            def scan_inputs(k):
                b_t, d_t = bcd[:, k.slot, 0, :], bcd[:, k.slot, 2, :]
                dve.wait_ge(bcd_copied, k.n + 1)
                dve.tensor_scalar(keep_h[:, k.slot, :], d_t, -1.0 / D, 1.0, ALU.mult, ALU.add).then_inc(keep_ready, 1)
                dve.scalar_tensor_tensor(drive[:, k.slot, :], d_t, 1.0 / D, b_t, ALU.mult, ALU.mult).then_inc(drive_ready, 1)

            def scan(k):
                dve.wait_ge(keep_ready, k.n + 1)
                dve.wait_ge(drive_ready, k.n + 1)
                dve.tensor_tensor_scan(hs[:, k.slot, :], keep_h[:, k.slot, :], drive[:, k.slot, :],
                                       hs[:, 1 - k.slot, P - 1:P], ALU.mult, ALU.add).then_inc(h_ready, 1)

            def scan_times_c(k):
                c_t = bcd[:, k.slot, 1, :]
                dve.wait_ge(h_ready, k.n + 1)
                wait(dve, s_ready, k.n - 1)
                dve.tensor_tensor(hc[:, k.slot, :], hs[:, k.slot, :], c_t, ALU.mult).then_inc(hc_ready, 1)

            def copy_s(k):
                dve.wait_ge(s_ready, k.n + 1)
                dve.tensor_copy(s_tok[:, k.slot, :], ps[:, 7, 0:NB]).then_inc(s_copied, 1)

            def residual_stats(k):
                dve.wait_ge(s_copied, k.n + 1)
                dve.wait_ge(xbo_ready, (k.n + 1) * 2)
                wait(dve, norm_ready, (k.n - 1) * NB)
                wait(dve, logits_ready, k.n - 1)
                routing = route(k.plus(-1)) if k.plus(-1).within(0, CH) else [lambda: None] * NB
                for b in range(NB):
                    dve.wait_ge(wo_ready, k.n * NB + b // 2 * 2 + 2)
                    dve.scalar_tensor_tensor(x1p[:, k.slot, b, :], ps[:, 2 + 2 * k.slot + b // 2, b % 2 * D:(b % 2 + 1) * D],
                                             s_tok[:, k.slot, b:b + 1], xbo[:, k.slot, b, :], ALU.mult, ALU.add).then_inc(x1p_ready, 1)
                    if b == 0 and k.plus(-1).within(0, CH):
                        route_logit(k.plus(-1))
                    routing[b]()
                for b in range(NB):
                    dve.wait_ge(x1p_ready, k.n * NB + b + 1)
                    dve.bn_stats(stats[:, k.slot, b, :], x1p[:, k.slot, b, :]).then_inc(stats_ready, 1)

            def mean_var(k):
                for b in range(NB):
                    dve.bn_aggr(mv[:, k.slot, b, :], stats[:, k.slot, b, :]).then_inc(mv_ready, 1)

            def variance_eps(k):
                dve.wait_ge(mv_ready, (k.n + 1) * NB)
                dve.tensor_scalar(var_eps[:, k.slot, :], mv[:, k.slot, :, 1], EPS, None, ALU.add).then_inc(var_ready, 1)

            def neg_mean_rstd(k):
                dve.wait_ge(rstd_ready, k.n + 1)
                dve.scalar_tensor_tensor(nmr[:, k.slot, :], mv[:, k.slot, :, 0], -1.0, rstd[:, k.slot, :], ALU.mult, ALU.mult)\
                   .then_inc(nmr_ready, 1)

            falls = falling[:, :].rearrange("p (a e) -> p a e", a=1).broadcast_to([P, NB, E])

            def per_expert(v):
                return v.rearrange("p (b a) -> p b a", a=1).broadcast_to([P, NB, E])

            def route_top(k):
                dve.wait_ge(logits_ready, k.n + 1)
                dve.reduce_max(top[:, k.slot, :], logits[:, k.slot, :, :], X_AXIS).then_inc(top_ready, 1)

            def route_logit(k):
                dve.wait_ge(rstd_ready, k.n + 1)
                dve.wait_ge(top_ready, k.n + 1)
                dve.tensor_tensor(rw_t[:, k.slot, :], top[:, k.slot, :], rstd[:, k.slot, :], ALU.mult).then_inc(rw_t_ready, 1)

            def route_cand(k):
                dve.wait_ge(top_ready, k.n + 1)
                dve.tensor_tensor(candidates[:, k.slot, :, :], logits[:, k.slot, :, :], per_expert(top[:, k.slot, :]), ALU.is_ge)\
                   .then_inc(cand_ready, 1)

            def route_first(k):
                dve.wait_ge(cand_ready, k.n + 1)
                dve.tensor_tensor(candidates[:, k.slot, :, :], candidates[:, k.slot, :, :], falls, ALU.mult).then_inc(first_ready, 1)

            def route_pick(k):
                dve.wait_ge(first_ready, k.n + 1)
                dve.reduce_max(pick[:, k.slot, :], candidates[:, k.slot, :, :], X_AXIS).then_inc(pick_ready, 1)

            def route_onehot(k):
                dve.wait_ge(pick_ready, k.n + 1)
                wait(dve, ranks_ready, k.n - 1)
                wait(dve, place_ready, k.n - 1)
                dve.tensor_tensor(picked[:, k.slot, 1:1 + NB, :], falls, per_expert(pick[:, k.slot, :]), ALU.is_equal).then_inc(onehot_ready, 1)

            def route(k):
                return [lambda: route_cand(k), lambda: route_first(k), lambda: route_pick(k), lambda: route_onehot(k)]

            def route_last(k):
                for part in (route_cand, route_first, route_pick, neg_mean_rstd, route_logit, route_onehot):
                    part(k)

            def route_earlier(k):
                dve.wait_ge(onehot_ready, k.n + 1)
                wait(dve, ranks_ready, k.n)
                with nc.allow_low_precision(reason="whole numbers below 2048 are exact in float32r"):
                    dve.reduce_sum(picked[:, 1 - k.slot, 0, :], picked[:, k.slot, :, :].bitcast(fp32).rearrange("p b e -> p e b"), X_AXIS)\
                       .then_inc(earlier_ready, 1)

            def router_weight_1(k):
                dve.wait_ge(rw_exp_ready, k.n + 1)
                dve.tensor_scalar_add(rw_1[:, k.slot, :], rw_e[:, k.slot, :], 1.0).then_inc(rw_1_ready, 1)

            def router_weight(k):
                dve.wait_ge(rw_1_ready, k.n + 1)
                wait(dve, rows_scattered[k.slot], 16 * NB * k.round)
                dve.reciprocal(rows[:, k.slot, :, D], rw_1[:, k.slot, :]).then_inc(rw_ready, 1)
                numbers = rows[:, k.slot, :, token_col].bitcast(i32)
                dve.tensor_scalar(numbers, numbers, R1 * P, None, ALU.add).then_inc(token_ready, 1)

            def places(k):
                dve.wait_ge(ranks_ready, k.n + 1)
                wait(dve, dest_f_ready, k.n)
                dve.tensor_tensor(place[:, k.slot, :, :], ps[:, 7, RANKS:RANKS + NB * E].rearrange("p (b e) -> p b e", e=E),
                                  picked[:, k.slot, 1:1 + NB, :].bitcast(fp32), ALU.mult).then_inc(place_ready, 1)

            def destinations(k):
                dve.wait_ge(place_ready, k.n + 1)
                dve.reduce_sum(dest_f[:, k.slot, :], place[:, k.slot, :, :], X_AXIS).then_inc(dest_f_ready, 1)

            def integer_destinations(k):
                dve.wait_ge(dest_f_ready, k.n + 1)
                wait(dve, rows_scattered[k.slot], 16 * NB * k.round)
                dve.tensor_copy(dest[:, k.slot, :], dest_f[:, k.slot, :]).then_inc(dest_ready, 1)

            def split_here(k):
                return k.within(1, CH)

            def add_bo(k):
                dve.wait_ge(x_loaded[k.slot], 16 * (k.round + 1))
                dve.wait_ge(x1p_ready, (k.n - 1) * NB)
                dve.tensor_tensor(xbo[:, k.slot, :, :], xr[:, k.slot, :, :],
                                  bo_row[:, :].rearrange("p (a d) -> p a d", a=1).broadcast_to([P, NB, D]), ALU.add).then_inc(xbo_ready, 2)

            def step(k):
                f, ff, p1, p2 = k.plus(1), k.plus(2), k.plus(-1), k.plus(-2)
                front, back = f.within(0, CH), k.within(0, CH)
                if split_here(ff):
                    split_hi(ff)
                if p2.within(0, CH):
                    places(p2)
                if split_here(ff):
                    split_lo(ff)
                if on_idle_vector(f):
                    add_bo(f)
                if p2.within(0, CH):
                    destinations(p2)
                if back:
                    scan_inputs(k)
                    scan(k)
                if p2.within(0, CH):
                    integer_destinations(p2)
                if back:
                    scan_times_c(k)
                if p1.within(0, CH) and back:
                    neg_mean_rstd(p1)
                if front:
                    abs_z(f, 1)
                if back:
                    copy_s(k)
                if front:
                    wait(dve, bcd_ready, f.n - 1)
                    dve.tensor_copy(bcd_tok[:, f.slot, 0:2, :].rearrange("p c (b n) -> p c b n", n=N),
                                    zs[:, f.slot, :, D:G0].rearrange("p b (c n) -> p c b n", n=N)).then_inc(delta_ready, 1)
                if p1.within(0, CH):
                    route_top(p1)
                if back:
                    residual_stats(k)
                elif p1.within(0, CH):
                    route_last(p1)
                if front:
                    dve.wait_ge(soft_ready, (f.n + 1) * 2)
                    dve.tensor_tensor(bcd_tok[:, f.slot, 2, :].rearrange("p (b n) -> p b n", n=N),
                                      relu_sum[:, f.slot, :].rearrange("p (b a) -> p b a", a=1).broadcast_to([P, NB, N]),
                                      ln_sum[:, f.slot, :].rearrange("p (b a) -> p b a", a=1).broadcast_to([P, NB, N]),
                                      ALU.add).then_inc(delta_ready, 1)
                if p1.within(0, CH):
                    route_earlier(p1)
                if isinstance(k.n, int) and k.n == CH:
                    dve.wait_ge(ends_ready, 1)
                    dve.tensor_copy(ends_i[:, :], ps[:, 0, 0:E]).then_inc(ends_i_ready, 1)
                if p1.within(0, CH):
                    router_weight_1(p1)
                if back and ff.within(0, CH):
                    dve.wait_ge(stats_ready, (k.n + 1) * NB)
                if ff.within(0, CH):
                    abs_z(ff, 0)
                if back:
                    if not ff.within(0, CH):
                        dve.wait_ge(stats_ready, (k.n + 1) * NB)
                    mean_var(k)
                if p1.within(0, CH):
                    router_weight(p1)
                if back:
                    variance_eps(k)

            step(Step(0, -2, R1))
            dve.wait_ge(setup_act, 1)
            link(dve.tensor_scalar_add(sig_a[:, 1:2], sig_a[:, 0:1], 1.0))
            link(dve.reciprocal(sig_a[:, 0:1], sig_a[:, 1:2]))
            dve.tensor_scalar(batch_sel[:, :], batch_sel[:, :], sig_a[:, 0:1], None, ALU.mult).then_inc(setup_dve, 1)
            run_steps(dve, step, -1, *LOOP1, CH + 2, R1)

            link(dve.tensor_scalar(tiles_i[:, :], ps[:, 0, 0:E], float(P - 1), None, ALU.add))
            link(dve.tensor_scalar(tiles_i[:, :], tiles_i[:, :], P.bit_length() - 1, None, ALU.logical_shift_right))
            link(dve.tensor_copy(tiles_f[:, :], tiles_i[:, :]))
            link(dve.tensor_tensor(tiles_f[:, :], tiles_f[:, :], region[:, :], ALU.subtract))
            link(dve.tensor_tensor_scan(tiles_in[:, :], ones[:, 0:E], tiles_f[:, :], 0.0, ALU.mult, ALU.add))
            link(dve.tensor_scalar(gap[:, :], tiles_f[:, :], -1.0, float(REGION), ALU.mult, ALU.add))
            per_tile = "p (a e) -> p a e"
            link(dve.tensor_tensor(past[:, :, :], tile_no[:, :].rearrange("p (t a) -> p t a", a=1).broadcast_to([1, ST, E]),
                                   tiles_in[0:1, :].rearrange(per_tile, a=1).broadcast_to([1, ST, E]), ALU.is_ge))
            link(dve.tensor_tensor(past_gap[:, :, :], past[:, :, :], gap[0:1, :].rearrange(per_tile, a=1).broadcast_to([1, ST, E]), ALU.mult))
            link(dve.reduce_sum(source_f[:, :], past_gap[:, :, :], X_AXIS))
            link(dve.tensor_tensor(source_f[:, :], source_f[:, :], tile_no[:, :], ALU.add))
            dve.tensor_scalar(source[:, :], source_f[:, :], float(E * REGION), None, ALU.min).then_inc(source_ready, 1)
            link(dve.reduce_sum(expert_f[:, :], past[:, :, :], X_AXIS))
            dve.tensor_scalar(expert[:, :], expert_f[:, :], float(E - 1), None, ALU.min).then_inc(expert_ready, 1)

            def ffn_step(t):
                cur, res, old = t, t.plus(-RES_LAG), t.plus(-LN_LAG)
                if res.within(0, ST):
                    r = res.c % R3
                    dve.wait_ge(y_ready, res.n + 1)
                    wait(dve, fout_ready, res.n + 1 - R3)
                    dve.tensor_tensor(x2p[:, r, :], ps[:, 6 + res.c % 2, 0:D], fr[:, res.slot, 0:D], ALU.add).then_inc(x2p_ready, 1)
                    wait(dve, out_stored[res.slot], 16 * res.round)
                    dve.tensor_copy(token[:, res.slot:res.slot + 1], fr[:, res.slot, token_col:token_col + 1].bitcast(i32)).then_inc(tok_ready, 1)
                    dve.wait_ge(x2p_ready, res.n + 1)
                    dve.bn_stats(fst[:, r, :], x2p[:, r, :]).then_inc(fst_ready, 1)
                if old.within(0, ST):
                    r = old.c % R3
                    dve.wait_ge(frs_ready, old.n + 1)
                    wait(dve, fout_ready, old.n + 1 - R3)
                    dve.scalar_tensor_tensor(fnm[:, r:r + 1], fmv[:, r, 0:1], -1.0, frs[:, r:r + 1], ALU.mult, ALU.mult)\
                       .then_inc(fnm_ready, 1)
                if res.within(0, ST):
                    dve.wait_ge(fst_ready, res.n + 1)
                if cur.within(0, ST):
                    dve.wait_ge(silu_ready, cur.n + 1)
                    wait(dve, hidt_ready, cur.n - 1)
                    dve.scalar_tensor_tensor(hid[:, cur.c % 2, :], ps[:, cur.c % 2, F:2 * F], fr[:, cur.slot, D:D + 1],
                                             silu_g[:, cur.c % 2, :], ALU.mult, ALU.mult).then_inc(hid_ready, 1)
                if res.within(0, ST):
                    r = res.c % R3
                    dve.bn_aggr(fmv[:, r, :], fst[:, r, :]).then_inc(fmv_ready, 1)
                    dve.wait_ge(fmv_ready, res.n + 1)
                    dve.tensor_scalar(fve[:, r:r + 1], fmv[:, r, 1:2], EPS, None, ALU.add).then_inc(fve_ready, 1)

            run_steps(dve, ffn_step, 0, *LOOP2, ST + LN_LAG, R2)

        @block.tensor
        def _(pe):
            def warm_up(products):
                for _ in range(products):
                    pe.matmul(ps[:, 5, 0:P], ones[:, :], ident[:, :], start=True, stop=True)

            pe.wait_ge(consts_ready, 13)
            warm_up(8)
            pe.wait_ge(gate_loaded, 16)
            for ic in range(KC):
                for jc in range(KC):
                    mm = pe.matmul(ps[:, ic, 0:E], wot_f[:, jc, ic * P:(ic + 1) * P], gwt_f[:, jc, :], start=(jc == 0), stop=(jc == KC - 1))
            mm.then_inc(setup_mm, 1)
            for jc in range(KC):
                pe.matmul(ps[:, 2, 0:E], ones[:, :], gwt_f[:, jc, :], start=(jc == 0), stop=(jc == KC - 1))
            pe.wait_ge(setup_dve, 5)
            for jc in range(KC):
                mm = pe.matmul(ps[:, 3, 0:E], ones[:, :], bogw[:, jc, :], start=(jc == 0), stop=(jc == KC - 1))
            mm.then_inc(setup_mm, 1)
            pe.wait_ge(setup_dve, 9)

            def products(dst, k, b, w_hi, w_lo, bias):
                tok = slice(b * P, (b + 1) * P)
                terms = [(xh, w_hi), (xh, w_lo), (xl, w_hi)]
                for i, (xs, w) in enumerate(terms):
                    for kc in range(KC):
                        mm = pe.matmul(dst, xs[:, k.slot, kc, tok], w[:, kc, :], start=(i == 0 and kc == 0),
                                       stop=(not bias and i == len(terms) - 1 and kc == KC - 1))
                if bias:
                    if isinstance(k.n, int) and k.n == 0 and b == 0:
                        pe.wait_ge(setup_dve, 12)
                    mm = pe.matmul(dst, two_ones[:, :], bias_hl[:, :], start=False, stop=True)
                return mm

            def tile_pair(k, p):
                if p == 0:
                    pe.wait_ge(xh_ready, k.n + 1)
                    pe.wait_ge(xl_ready, k.n + 1)
                for b in (2 * p, 2 * p + 1):
                    wait(pe, z_copied, k.n * 2 + p)
                    products(ps[:, b % 2, 0:ZS], k, b, wz_hi, wz_lo, True).then_inc(z_ready, 1)
                if isinstance(k.n, int) and k.n == 0 and p == 0:
                    pe.wait_ge(setup_dve, 13)
                wait(pe, x1p_ready, (k.n - 2) * NB + 2 * p + 2)
                for b in (2 * p, 2 * p + 1):
                    products(ps[:, 2 + 2 * k.slot + p, b % 2 * D:(b % 2 + 1) * D], k, b, wo_hi, wo_lo, False).then_inc(wo_ready, 1)

            def ranks(k):
                pe.wait_ge(onehot_ready, k.n + 1)
                wait(pe, earlier_ready, k.n)
                wait(pe, place_ready, k.n)
                at = ps[:, 7, RANKS:RANKS + NB * E].rearrange("p (b e) -> p b e", e=E)
                pe.matmul(at, below_r[:, :], picked[:, k.slot, 1:1 + NB, :], start=True, stop=False)
                for b in range(NB):
                    mm = pe.matmul(at[:, b:NB, :], ones_r[:, :], picked[:, k.slot, b:b + 1, :].broadcast_to([P, NB - b, E]),
                                   start=False, stop=(b == NB - 1))
                mm.then_inc(ranks_ready, 1)

            def step(k):
                f, ff, p1 = k.plus(1), k.plus(2), k.plus(-1)
                front, back = f.within(0, CH), k.within(0, CH)
                if back:
                    pe.wait_ge(delta_ready, (k.n + 1) * 2)
                    wait(pe, bcd_copied, k.n)
                    pe.transpose(ps[:, 6, 0:P], bcd_tok[:, k.slot, 0:2, :].rearrange("p c q -> p (c q)"), ident[:, :])
                    for i in (1, 2):
                        tr = pe.transpose(ps[0:Q, 6, i * P:(i + 1) * P], bcd_tok[:, k.slot, i, :], ident[:, :])
                    tr.then_inc(bcd_ready, 1)
                if front:
                    tile_pair(f, 1)
                if back:
                    pe.wait_ge(hc_ready, k.n + 1)
                    wait(pe, s_copied, k.n)
                    wait(pe, place_ready, k.n - 1)
                    pe.matmul(ps[:, 7, 0:NB], hc[:, k.slot, :], batch_sel[:, :], start=True, stop=True).then_inc(s_ready, 1)
                if ff.within(0, CH):
                    tile_pair(ff, 0)
                if p1.within(0, CH):
                    wait(pe, s_copied, k.n + 1 if back else CH)
                    ranks(p1)

            step(Step(0, -2, R1))
            pe.wait_ge(a_loaded, 16)
            for jc in range(KC):
                mm = pe.matmul(ps[0:Q, 7, 0:1], a4[:, jc, :, :].rearrange("p b n -> p (b n)"), ones[:, 0:1], start=(jc == 0), stop=(jc == KC - 1))
            mm.then_inc(setup_mm, 1)
            run_steps(pe, step, -1, *LOOP1, CH, R1)
            pe.wait_ge(earlier_ready, CH)
            pe.matmul(ps[:, 0, 0:E], ones_r[:, :], picked[:, CH % R1, 0, :], start=True, stop=True).then_inc(ends_ready, 1)
            step(Step(0, CH, R1))

            pe.wait_ge(expert_ready, 1)
            pe.wait_ge(moe_loaded, 32 * CH)
            for s in range(R1):
                pe.wait_ge(rows_scattered[s], 16 * NB * CH // R1)
            warm_up(6)

            experts = {}

            def load_expert(j):
                stretch = (isinstance(j.n, int), j.c)
                if stretch not in experts:
                    experts[stretch] = nc.s_assert_within(pe.value_load(expert[0:1, bass.ds(j.n, 1)]), 0, E - 1,
                                                          skip_runtime_bounds_check_because="a count of experts, cut off at E - 1")
                return experts[stretch]

            def ffn_step(t):
                cur, nxt, prev, old = t, t.plus(1), t.plus(-2), t.plus(-3)
                if old.within(0, ST):
                    e_old = load_expert(old)
                if cur.within(0, ST):
                    e_cur = load_expert(cur)
                if nxt.within(0, ST):
                    h = nxt.c % 2
                    pe.wait_ge(fr_loaded[nxt.slot], 16 * (nxt.round + 1))
                    wait(pe, fxt_copied, nxt.n - 1)
                    for kc in range(KC):
                        tr = pe.transpose(ps[:, 2 + h, kc * P:(kc + 1) * P], fr[:, nxt.slot, kc * P:(kc + 1) * P], ident[:, :])
                    tr.then_inc(fxt_ready, 1)
                if prev.within(0, ST):
                    h = prev.c % 2
                    pe.wait_ge(hid_ready, prev.n + 1)
                    wait(pe, hidt_copied, prev.n - 1)
                    pe.transpose(ps[:, 4 + h, 0:P], hid[:, h, :], ident[:, :]).then_inc(hidt_ready, 1)
                if old.within(0, ST):
                    h = old.c % 2
                    pe.wait_ge(hidt_copied, old.n + 1)
                    wait(pe, x2p_ready, old.n - 1)
                    pe.matmul(ps[:, 6 + h, 0:D], hidt[:, h, :], w_dn[:, bass.ds(e_old, 1), :].rearrange("p a n -> p (a n)"),
                              start=True, stop=True).then_inc(y_ready, 1)
                if cur.within(0, ST):
                    h = cur.c % 2
                    pe.wait_ge(fxt_copied, cur.n + 1)
                    wait(pe, hid_ready, cur.n - 1)
                    for kc in range(KC):
                        mm = pe.matmul(ps[:, h, 0:2 * F], fxt[:, cur.c % R3, kc, :], w_gu[:, bass.ds(e_cur, 1), kc, :].rearrange("p a n -> p (a n)"),
                                       start=(kc == 0), stop=(kc == KC - 1))
                    mm.then_inc(gu_ready, 1)

            run_steps(pe, ffn_step, -1, *LOOP2, ST + 3, R2)


def kernel(**inputs):
    import numpy as _np
    import concourse.bacc as _bacc
    from concourse import mybir as _mybir
    from concourse.bass_utils import run_bass_kernel_spmd as _run

    i = {k.removeprefix("L0_"): _np.asarray(v) for k, v in inputs.items()}
    x = i["attn_x"]
    nb, t, d = x.shape
    p = 128
    n_exp, f, _ = i["ffn_w_gate"].shape
    xt = x.reshape(nb, t // p, p, d // p, p).transpose(1, 4, 3, 0, 2).reshape(t // p, p, d // p, nb * p)
    wgu = _np.stack([i["ffn_w_gate"], i["ffn_w_up"]], axis=1)
    wgu = wgu.reshape(n_exp, 2, f, d // p, p).transpose(4, 0, 3, 1, 2).reshape(p, n_exp, d // p, 2 * f)
    gate_pack = _np.concatenate([i["attn_Wo"].T, i["ffn_gate_w"].T, i["attn_bo"][:, None]], axis=1)
    bias_row = _np.concatenate([i["attn_bd"], i["attn_bb"], i["attn_bc"]])
    given = {
        "x": x, "xt": xt, "wdbc": _np.concatenate([i["attn_Wd"], i["attn_Wb"], i["attn_Wc"]], axis=1), "wo": i["attn_Wo"], "gate_pack": gate_pack,
        "bias_rows": _np.stack([bias_row, bias_row]), "bo": i["attn_bo"], "a_tiled": _np.repeat(i["attn_A"][:, None, :], nb, axis=1),
        "wgu": wgu, "wdn": i["ffn_w_down"].transpose(0, 2, 1),
    }
    nc = _bacc.Bacc("TRN2", target_bir_lowering=False, num_devices=1)
    arrays, args = {}, {}
    for name, a in given.items():
        a = _np.ascontiguousarray(a)
        arrays[f"in_{name}"] = a
        args[name] = nc.dram_tensor(f"in_{name}", a.shape, _mybir.dt.from_np(a.dtype), kind="ExternalInput").ap()
    args["out"] = nc.dram_tensor("out", (nb * t, d), _mybir.dt.float32, kind="ExternalOutput").ap()
    ssm_attention_then_top1_moe(nc, **args)
    r = _run(nc, [arrays], core_ids=[0])
    return r.results[0]["out"].reshape(nb, t, d)
```
